# Optimizing a Trainium2 kernel written in Bass

```python
import numpy as np
import jax
import jax.numpy as jnp

def _softmax(x, axis=-1):
    return jax.nn.softmax(x, axis=axis)

def _gelu(x):
    return jax.nn.gelu(x, approximate=True)

def _silu(x):
    return jax.nn.silu(x)

def _sigmoid(x):
    return jax.nn.sigmoid(x)

def _layernorm(x, axis=-1, eps=1e-05):
    m = jnp.mean(x, axis=axis, keepdims=True)
    v = jnp.var(x, axis=axis, keepdims=True)
    return (x - m) / jnp.sqrt(v + eps)

def _scatter_add(tgt, idx, src, axis=0):
    return tgt.at[idx].add(src)

def _segment_sum(src, seg, n):
    return jax.ops.segment_sum(src, seg, n)
kernel_name = 'mk_flamingo_gated_d2_seqx_r4_55ee1b'

def setup_inputs(seed: int=0):
    np.random.seed(seed)
    _w = jnp.asarray

    def _rec_inputs():
        import jax
        import jax.numpy as jnp
        _rk = jax.random.key(seed)
        x = -0.0005207 + 1.001 * jax.random.normal(jax.random.fold_in(_rk, 1), (4, 512, 256), jnp.float32)
        _lenS = 512 - jax.random.randint(jax.random.fold_in(_rk, 7), (4,), 0, max(1, 512 // 4) + 1, jnp.int32)
        _lenS2 = 512 - jax.random.randint(jax.random.fold_in(_rk, 8), (4,), 0, max(1, 512 // 4) + 1, jnp.int32)
        _ctx_1024P = jax.random.normal(jax.random.fold_in(_rk, 11), (4, 16, 256), jnp.float32)
        _ctx_1024c = jax.random.dirichlet(jax.random.fold_in(_rk, 511), 0.3 * jnp.ones((16,), jnp.float32), (4, 512))
        _ctx_1024t = jnp.einsum('bsk,bkd->bsd', _ctx_1024c, _ctx_1024P)
        _ctx_1024t = _ctx_1024t * jax.lax.rsqrt(jnp.mean(jnp.square(_ctx_1024t)) + 1e-12) * 0.953939
        ctx_1024 = -0.000514642 + 1.00011 * (_ctx_1024t + 0.3 * jax.random.normal(jax.random.fold_in(_rk, 611), (4, 512, 256), jnp.float32))
        _validS = jnp.arange(512)[None, :] < _lenS[:, None]
        _validS2 = jnp.arange(512)[None, :] < _lenS2[:, None]
        _causal = jnp.tril(jnp.ones((512, 512), dtype=bool))
        mask_BxS2_ik0 = jnp.where(jnp.broadcast_to(_validS2[:, :], (4, 512)), 0, 1).astype(jnp.int32)
        _g = jax.random.normal(jax.random.fold_in(_rk, 9001), (2, 2), jnp.float32)
        _g = jnp.sign(_g) * jnp.maximum(jnp.abs(_g), 1.0) + (_g == 0) * 1.0
        g_xattn = _g[0]
        g_ffn = _g[1]
        return (x, ctx_1024, mask_BxS2_ik0, g_xattn, g_ffn)
    x, ctx_1024, mask_BxS2_ik0, g_xattn, g_ffn = _rec_inputs()

    def _L0_xattn_setup():
        import jax, jax.numpy as jnp
        import numpy as np
        D_MODEL = 256
        N_HEADS = 16
        D_HEAD = D_MODEL // N_HEADS
        NEG = 10000000.0

        def _rel_shift(rel, k_len):
            B, H, L, P = rel.shape
            shift = 1 + (L != k_len)
            rel = rel.reshape(B, H, P, L)
            rel = rel[:, :, shift:, :]
            rel = rel.reshape(B, H, L, P - shift)
            return rel[..., :k_len]
        key = jax.random.key(seed)
        ks = jax.random.split(key, 16)
        B, L, D, H, dh = (1, 512, D_MODEL, N_HEADS, D_HEAD)
        s = 0.02
        inp = {'q': jax.random.normal(ks[0], (B, L, D), jnp.float32), 'k': jax.random.normal(ks[1], (B, L, D), jnp.float32), 'v': jax.random.normal(ks[2], (B, L, D), jnp.float32), 'pos_enc': jax.random.normal(ks[3], (L + 1, D), jnp.float32), 'Wq': jax.random.normal(ks[4], (D, D), jnp.float32) * s, 'bq': jnp.zeros((D,), jnp.float32), 'Wk': jax.random.normal(ks[5], (D, D), jnp.float32) * s, 'bk': jnp.zeros((D,), jnp.float32), 'Wv': jax.random.normal(ks[6], (D, D), jnp.float32) * s, 'bv': jnp.zeros((D,), jnp.float32), 'Wo': jax.random.normal(ks[7], (D, D), jnp.float32) * s, 'bo': jnp.zeros((D,), jnp.float32), 'r_w_bias': jax.random.normal(ks[8], (H, 1, dh), jnp.float32) * s, 'r_r_bias': jax.random.normal(ks[9], (H, 1, dh), jnp.float32) * s, 'r_kernel': jax.random.normal(ks[10], (H, D, dh), jnp.float32) * s}
        return inp
    _L0_xattn_all = _L0_xattn_setup()
    _L0_xattn_in = {k: v for k, v in _L0_xattn_all.items() if k in ('pos_enc', 'Wq', 'bq', 'Wk', 'bk', 'Wv', 'bv', 'Wo', 'bo', 'r_w_bias', 'r_r_bias', 'r_kernel')}
    del _L0_xattn_all

    def _L0_ffn_setup():
        import jax, jax.numpy as jnp
        import numpy as np
        B, S, D, H, DOUT, E, K = (4, 512, 256, 256, 256, 8, 2)
        key = jax.random.key(seed)
        k1, k2, k3, k4 = jax.random.split(key, 4)
        x = jax.random.normal(k1, (B, S, D), dtype=jnp.float32)
        Wr = jax.random.normal(k2, (D, E), dtype=jnp.float32) * 0.02
        Wi = jax.random.normal(k3, (E, D, H), dtype=jnp.float32) * 0.02
        Wo = jax.random.normal(k4, (E, H, DOUT), dtype=jnp.float32) * 0.02
        return {'x': x, 'Wr': Wr, 'Wi': Wi, 'Wo': Wo}
    _L0_ffn_all = _L0_ffn_setup()
    _L0_ffn_in = {k: v for k, v in _L0_ffn_all.items() if k in ('Wr', 'Wi', 'Wo')}
    del _L0_ffn_all

    def _L1_xattn_setup():
        import math
        import jax, jax.numpy as jnp
        import numpy as np
        EMBED_DIM = 256
        NUM_HEADS = 16
        HEAD_DIM = EMBED_DIM // NUM_HEADS
        B, QLEN, KLEN = (2, 512, 512)
        key = jax.random.key(seed)
        ks = jax.random.split(key, 8)
        s = 1.0 / math.sqrt(EMBED_DIM)
        return {'query': jax.random.normal(ks[0], (B, QLEN, EMBED_DIM), dtype=jnp.float32), 'key': jax.random.normal(ks[1], (B, KLEN, EMBED_DIM), dtype=jnp.float32), 'val': jax.random.normal(ks[2], (B, KLEN, EMBED_DIM), dtype=jnp.float32), 'mask': jax.random.randint(ks[3], (B, KLEN), 0, 2, dtype=jnp.int32), 'Wq': jax.random.normal(ks[4], (EMBED_DIM, EMBED_DIM), dtype=jnp.float32) * s, 'Wk': jax.random.normal(ks[5], (EMBED_DIM, EMBED_DIM), dtype=jnp.float32) * s, 'Wv': jax.random.normal(ks[6], (EMBED_DIM, EMBED_DIM), dtype=jnp.float32) * s, 'Wo': jax.random.normal(ks[7], (EMBED_DIM, EMBED_DIM), dtype=jnp.float32) * s}
    _L1_xattn_all = _L1_xattn_setup()
    _L1_xattn_in = {k: v for k, v in _L1_xattn_all.items() if k in ('Wq', 'Wk', 'Wv', 'Wo')}
    del _L1_xattn_all

    def _L1_ffn_setup():
        import jax, jax.numpy as jnp
        import numpy as np
        S, B, H = (512, 1, 256)
        N_HEADS = 16
        HEAD_DIM = H // N_HEADS
        E, K, F = (8, 2, 512)
        EPS = 1e-05

        def layernorm(x, w, b):
            mu = jnp.mean(x, axis=-1, keepdims=True)
            var = jnp.mean(jnp.square(x - mu), axis=-1, keepdims=True)
            return (x - mu) * jax.lax.rsqrt(var + EPS) * w + b
        key = jax.random.key(seed)
        ks = jax.random.split(key, 8)
        std = 0.02
        return {'x': jax.random.normal(ks[0], (S, B, H), dtype=jnp.float32), 'ln1_w': jnp.ones((H,), jnp.float32), 'ln1_b': jnp.zeros((H,), jnp.float32), 'in_proj_w': jax.random.normal(ks[1], (3 * H, H), jnp.float32) * std, 'in_proj_b': jnp.zeros((3 * H,), jnp.float32), 'out_proj_w': jax.random.normal(ks[2], (H, H), jnp.float32) * std, 'out_proj_b': jnp.zeros((H,), jnp.float32), 'ln2_w': jnp.ones((H,), jnp.float32), 'ln2_b': jnp.zeros((H,), jnp.float32), 'router_w': jax.random.normal(ks[3], (E, H), jnp.float32) * std, 'w1': jax.random.normal(ks[4], (E, H, F), jnp.float32) * std, 'w2': jax.random.normal(ks[5], (E, F, H), jnp.float32) * std}
    _L1_ffn_all = _L1_ffn_setup()
    _L1_ffn_in = {k: v for k, v in _L1_ffn_all.items() if k in ('ln1_w', 'ln1_b', 'in_proj_w', 'in_proj_b', 'out_proj_w', 'out_proj_b', 'ln2_w', 'ln2_b', 'router_w', 'w1', 'w2')}
    del _L1_ffn_all
    return {'x': x, 'ctx_1024': ctx_1024, 'mask_BxS2_ik0': mask_BxS2_ik0, 'g_xattn': g_xattn, 'g_ffn': g_ffn, 'L0_xattn_pos_enc': _L0_xattn_in['pos_enc'], 'L0_xattn_Wq': _L0_xattn_in['Wq'], 'L0_xattn_bq': _L0_xattn_in['bq'], 'L0_xattn_Wk': _L0_xattn_in['Wk'], 'L0_xattn_bk': _L0_xattn_in['bk'], 'L0_xattn_Wv': _L0_xattn_in['Wv'], 'L0_xattn_bv': _L0_xattn_in['bv'], 'L0_xattn_Wo': _L0_xattn_in['Wo'], 'L0_xattn_bo': _L0_xattn_in['bo'], 'L0_xattn_r_w_bias': _L0_xattn_in['r_w_bias'], 'L0_xattn_r_r_bias': _L0_xattn_in['r_r_bias'], 'L0_xattn_r_kernel': _L0_xattn_in['r_kernel'], 'L0_ffn_Wr': _L0_ffn_in['Wr'], 'L0_ffn_Wi': _L0_ffn_in['Wi'], 'L0_ffn_Wo': _L0_ffn_in['Wo'], 'L1_xattn_Wq': _L1_xattn_in['Wq'], 'L1_xattn_Wk': _L1_xattn_in['Wk'], 'L1_xattn_Wv': _L1_xattn_in['Wv'], 'L1_xattn_Wo': _L1_xattn_in['Wo'], 'L1_ffn_ln1_w': _L1_ffn_in['ln1_w'], 'L1_ffn_ln1_b': _L1_ffn_in['ln1_b'], 'L1_ffn_in_proj_w': _L1_ffn_in['in_proj_w'], 'L1_ffn_in_proj_b': _L1_ffn_in['in_proj_b'], 'L1_ffn_out_proj_w': _L1_ffn_in['out_proj_w'], 'L1_ffn_out_proj_b': _L1_ffn_in['out_proj_b'], 'L1_ffn_ln2_w': _L1_ffn_in['ln2_w'], 'L1_ffn_ln2_b': _L1_ffn_in['ln2_b'], 'L1_ffn_router_w': _L1_ffn_in['router_w'], 'L1_ffn_w1': _L1_ffn_in['w1'], 'L1_ffn_w2': _L1_ffn_in['w2']}

def reference(x, ctx_1024, mask_BxS2_ik0, g_xattn, g_ffn, L0_xattn_pos_enc, L0_xattn_Wq, L0_xattn_bq, L0_xattn_Wk, L0_xattn_bk, L0_xattn_Wv, L0_xattn_bv, L0_xattn_Wo, L0_xattn_bo, L0_xattn_r_w_bias, L0_xattn_r_r_bias, L0_xattn_r_kernel, L0_ffn_Wr, L0_ffn_Wi, L0_ffn_Wo, L1_xattn_Wq, L1_xattn_Wk, L1_xattn_Wv, L1_xattn_Wo, L1_ffn_ln1_w, L1_ffn_ln1_b, L1_ffn_in_proj_w, L1_ffn_in_proj_b, L1_ffn_out_proj_w, L1_ffn_out_proj_b, L1_ffn_ln2_w, L1_ffn_ln2_b, L1_ffn_router_w, L1_ffn_w1, L1_ffn_w2):
    import jax
    import jax.numpy as jnp

    def _L0_xattn_ref(q, k, v, pos_enc, Wq, bq, Wk, bk, Wv, bv, Wo, bo, r_w_bias, r_r_bias, r_kernel):
        import jax, jax.numpy as jnp
        import numpy as np
        D_MODEL = 256
        N_HEADS = 16
        D_HEAD = D_MODEL // N_HEADS
        NEG = 10000000.0

        def _rel_shift(rel, k_len):
            B, H, L, P = rel.shape
            shift = 1 + (L != k_len)
            rel = rel.reshape(B, H, P, L)
            rel = rel[:, :, shift:, :]
            rel = rel.reshape(B, H, L, P - shift)
            return rel[..., :k_len]
        B, L, D = q.shape
        H, dh = (N_HEADS, D_HEAD)
        scale = dh ** (-0.5)
        qp = q @ Wq.T + bq
        kp = k @ Wk.T + bk
        vp = v @ Wv.T + bv
        split = lambda x: x.reshape(B, L, H, dh).transpose(0, 2, 1, 3)
        qh, kh, vh = (split(qp), split(kp), split(vp))
        scores = jnp.einsum('bhld,bhmd->bhlm', qh + r_w_bias, kh) * scale
        pe = jnp.einsum('pm,hmd->hpd', pos_enc, r_kernel)
        rel = jnp.einsum('bhld,hpd->bhlp', qh + r_r_bias, pe) * scale
        scores = scores + _rel_shift(rel, L)
        causal = jnp.triu(jnp.ones((L, L), jnp.float32), 1)
        scores = scores - causal * NEG
        attn = jax.nn.softmax(scores, axis=-1)
        out = jnp.einsum('bhlm,bhmd->bhld', attn, vh)
        out = out.transpose(0, 2, 1, 3).reshape(B, L, D)
        return out @ Wo.T + bo

    def _L0_ffn_ref(x, Wr, Wi, Wo):
        import jax, jax.numpy as jnp
        import numpy as np
        B, S, D, H, DOUT, E, K = (4, 512, 256, 256, 256, 8, 2)
        b, s, d = x.shape
        e_cnt, _, h = Wi.shape
        dout = Wo.shape[2]
        xf = x.reshape(-1, d)
        T = xf.shape[0]
        probs = jax.nn.softmax(xf @ Wr, axis=-1)
        topk_p, topk_i = jax.lax.top_k(probs, K)
        mask = topk_i[:, :, None] == jnp.arange(e_cnt)[None, None, :]
        hmix = jnp.zeros((T, K, h), dtype=xf.dtype)
        for e in range(e_cnt):
            he = xf @ Wi[e]
            hmix = hmix + jnp.where(mask[:, :, e][:, :, None], he[:, None, :], 0.0)
        o = jnp.zeros((T, K, dout), dtype=xf.dtype)
        for e in range(e_cnt):
            oe = jnp.einsum('tkh,hd->tkd', hmix, Wo[e])
            o = o + jnp.where(mask[:, :, e][:, :, None], oe, 0.0)
        out = jnp.sum(o * topk_p[:, :, None], axis=1)
        return out.reshape(b, s, dout)

    def _L1_xattn_ref(query, key, val, mask, Wq, Wk, Wv, Wo):
        import math
        import jax, jax.numpy as jnp
        import numpy as np
        EMBED_DIM = 256
        NUM_HEADS = 16
        HEAD_DIM = EMBED_DIM // NUM_HEADS
        B, QLEN, KLEN = (2, 512, 512)
        Bsz, Q, E = query.shape
        H, D = (NUM_HEADS, HEAD_DIM)
        q = (query @ Wq.T).reshape(Bsz, Q, H, D)
        k = (key @ Wk.T).reshape(Bsz, -1, H, D)
        v = (val @ Wv.T).reshape(Bsz, -1, H, D)
        logits = jnp.einsum('bqhd,bkhd->bhqk', q, k) / math.sqrt(E)
        logits = logits - mask.astype(logits.dtype)[:, None, None, :] * 10000.0
        probs = jax.nn.softmax(logits, axis=-1)
        out = jnp.einsum('bhqk,bkhd->bqhd', probs, v).reshape(Bsz, Q, E)
        return out @ Wo.T

    def _L1_ffn_ref(x, ln1_w, ln1_b, in_proj_w, in_proj_b, out_proj_w, out_proj_b, ln2_w, ln2_b, router_w, w1, w2):
        import jax, jax.numpy as jnp
        import numpy as np
        S, B, H = (512, 1, 256)
        N_HEADS = 16
        HEAD_DIM = H // N_HEADS
        E, K, F = (8, 2, 512)
        EPS = 1e-05

        def layernorm(x, w, b):
            mu = jnp.mean(x, axis=-1, keepdims=True)
            var = jnp.mean(jnp.square(x - mu), axis=-1, keepdims=True)
            return (x - mu) * jax.lax.rsqrt(var + EPS) * w + b
        s, b, h = x.shape
        hn = layernorm(x, ln1_w, ln1_b)
        qkv = hn @ in_proj_w.T + in_proj_b
        q, k, v = jnp.split(qkv, 3, axis=-1)
        q = q.reshape(s, b, N_HEADS, HEAD_DIM)
        k = k.reshape(s, b, N_HEADS, HEAD_DIM)
        v = v.reshape(s, b, N_HEADS, HEAD_DIM)
        scores = jnp.einsum('sbnd,tbnd->bnst', q, k) / np.sqrt(HEAD_DIM)
        causal = jnp.tril(jnp.ones((s, s), bool))
        scores = jnp.where(causal[None, None], scores, -jnp.inf)
        probs = jax.nn.softmax(scores, axis=-1)
        attn = jnp.einsum('bnst,tbnd->sbnd', probs, v).reshape(s, b, h)
        attn = attn @ out_proj_w.T + out_proj_b
        x1 = x + attn
        hn2 = layernorm(x1, ln2_w, ln2_b).reshape(s * b, h)
        logits = hn2 @ router_w.T
        rp = jax.nn.softmax(logits, axis=-1)
        topw, topi = jax.lax.top_k(rp, K)
        gates = jnp.sum(jax.nn.one_hot(topi, E, dtype=hn2.dtype) * topw[..., None], axis=1)
        hmid = jax.nn.gelu(jnp.einsum('th,ehf->tef', hn2, w1), approximate=False)
        y = jnp.einsum('tef,efh->th', hmid * gates[:, :, None], w2)
        return x1 + y.reshape(s, b, h)
    x = x + jnp.tanh(g_xattn[0]) * _L0_xattn_ref(_layernorm(x, axis=-1), ctx_1024, ctx_1024, L0_xattn_pos_enc, L0_xattn_Wq, L0_xattn_bq, L0_xattn_Wk, L0_xattn_bk, L0_xattn_Wv, L0_xattn_bv, L0_xattn_Wo, L0_xattn_bo, L0_xattn_r_w_bias, L0_xattn_r_r_bias, L0_xattn_r_kernel)
    x = x + jnp.tanh(g_ffn[0]) * _L0_ffn_ref(_layernorm(x, axis=-1), L0_ffn_Wr, L0_ffn_Wi, L0_ffn_Wo)
    x = x + jnp.tanh(g_xattn[1]) * _L1_xattn_ref(_layernorm(x, axis=-1), ctx_1024, ctx_1024, mask_BxS2_ik0, L1_xattn_Wq, L1_xattn_Wk, L1_xattn_Wv, L1_xattn_Wo)
    x = x + jnp.tanh(g_ffn[1]) * _L1_ffn_ref(_layernorm(x, axis=-1), L1_ffn_ln1_w, L1_ffn_ln1_b, L1_ffn_in_proj_w, L1_ffn_in_proj_b, L1_ffn_out_proj_w, L1_ffn_out_proj_b, L1_ffn_ln2_w, L1_ffn_ln2_b, L1_ffn_router_w, L1_ffn_w1, L1_ffn_w2)
    return x

_drawn_inputs = setup_inputs


def setup_inputs(seed=0):
    import zlib

    import numpy as np

    out = dict(_drawn_inputs(seed))
    spreads = {'g_ffn': (-1.0, 0.2),
     'L0_xattn_bq': (0.0, 0.8),
     'L0_xattn_bk': (0.0, 2.0),
     'L0_xattn_bv': (0.0, 0.335),
     'L0_xattn_bo': (0.0, 0.1),
     'L1_ffn_ln1_w': (1.0, 0.2),
     'L1_ffn_ln1_b': (0.0, 0.29),
     'L1_ffn_in_proj_b': (0.0, 0.1),
     'L1_ffn_out_proj_b': (0.0, 0.1),
     'L1_ffn_ln2_w': (1.0, 0.6),
     'L1_ffn_ln2_b': (0.0, 0.45)}
    factors = {'L0_xattn_pos_enc': 8.0,
     'L0_xattn_Wq': 8.0,
     'L0_xattn_Wk': 8.0,
     'L0_xattn_r_w_bias': 47.859,
     'L0_xattn_r_r_bias': 8.0,
     'L0_xattn_r_kernel': 8.0,
     'L0_ffn_Wr': 3.509,
     'L0_ffn_Wi': 3.082,
     'L0_ffn_Wo': 3.094}
    for name, (base, spread) in spreads.items():
        noise = np.random.default_rng([zlib.crc32(name.encode()), seed]).standard_normal(out[name].shape)
        drawn = base * np.exp(spread * noise) if base else spread * noise
        out[name] = jnp.asarray(drawn.astype(out[name].dtype))
    for name, factor in factors.items():
        out[name] = (out[name] * factor).astype(out[name].dtype)
    return out
```

```python
from contextlib import ExitStack

import concourse.bass as bass
from concourse import mybir

F32 = mybir.dt.float32
BF16 = mybir.dt.bfloat16
I32 = mybir.dt.int32
ALU = mybir.AluOpType
ACT = mybir.ActivationFunctionType
AX = mybir.AxisListType

P = 128
B, L, D = 4, 512, 256
H, DH = 16, 16
E, TOP = 8, 2
F = 512
KC = D // P
LT = L // P
NT = B * LT
HG = 4
NG = B * (H // HG)
EPS = 1e-5
NEG = -10000000.0
LEAST = -3.0e38
PARTS = 3
RUNS = [(0, 0, 3), (0, 1, 2), (0, 2, 1)]
SROWS = sum(n for _, _, n in RUNS) * DH


class Count:

    def __init__(self, n, it=None, per=4):
        self.n, self.it, self.per = n, it, per

    def shift(self, d):
        return Count(self.n + d, self.it, self.per)

    def value(self, k=1, c=0):
        static = k * self.n + c
        return static if self.it is None else self.it * (self.per * k) + static

    def slot(self, ring):
        return self.n % ring

    def uses(self, ring, k=1, c=0):
        static = k * (self.n // ring) + c
        return static if self.it is None else self.it * (self.per // ring * k) + static

    def wait(self, eng, sem, k=1, c=0, apart=None):
        self._wait(eng, sem, self.value(k, c), k * self.n + c, apart)

    def wait_uses(self, eng, sem, ring, k=1, c=0, apart=None):
        self._wait(eng, sem, self.uses(ring, k, c), k * (self.n // ring) + c, apart)

    def _wait(self, eng, sem, value, first, apart=None):
        if self.it is None and first <= 0:
            return
        assert first > 0, "a wait in a loop has to be positive from the first round on"
        eng.wait_ge(sem, value)
        if apart is not None and self.it is not None:
            eng.sem_inc(apart, 1)


class Phase:

    def __init__(self, nc, name):
        self.nc, self.name, self.stack, self.held = nc, name, ExitStack(), []

    def __enter__(self):
        self.stack.__enter__()
        self.stack.callback(self._clear)
        return self

    def _clear(self):
        if self.held:
            self.nc.clear_and_free_semaphores(self.held)
            self.nc.all_engine_barrier()

    def __exit__(self, *a):
        return self.stack.__exit__(*a)

    def sb(self, name, shape, dt=F32):
        return self.stack.enter_context(self.nc.sbuf_tensor(f"{self.name}_{name}", shape, dt))

    def ps(self, name, shape, dt=F32):
        return self.stack.enter_context(self.nc.psum_tensor(f"{self.name}_{name}", shape, dt))

    def sem(self, name):
        self.held.append(self.nc.alloc_semaphore(f"{self.name}_{name}"))
        return self.held[-1]

    def sems(self, name, n):
        return [self.sem(f"{name}{i}") for i in range(n)]

    def block(self):
        return self.stack.enter_context(self.nc.Block())


def batches(eng):
    with eng.Fori(0, B // 2) as it:
        for par in range(2):
            yield Count(par, it, per=2)


def row_of(v, parts=P):
    n = v.shape[0]
    return bass.AP(v.tensor, v.offset, [[0, parts], [1, n]])


REL_SLOTS = 4
NEG_WRITES = REL_SLOTS * LT


def constants(nc, io, keep, scr):
    with Phase(nc, "const") as ph:
        gates = ph.sb("gates", [P, 4])
        zeroed, identity_ready, gates_loaded, tanh_ready = map(ph.sem, ["zeroed", "ident", "gates_loaded", "tanh"])
        negs_set = ph.sem("negs_set")
        block = ph.block()

        @block.gpsimd
        def _(pool):
            pool.memset(keep.negs[:, :], NEG).then_inc(negs_set, 1)
            pool.memset(keep.ident[:, :], 0.0).then_inc(zeroed, 1)
            pool.memset(keep.identb[:, :], 0.0).then_inc(zeroed, 1)
            pool.wait_ge(zeroed, 2)
            for m in (keep.ident, keep.identb):
                pool.affine_select(out=m[:, :], in_=m[:, :], compare_op=ALU.not_equal, fill=1.0, base=0,
                                   pattern=[[-1, P]], channel_multiplier=1).then_inc(identity_ready, 1)

        @block.sync
        def _(sp):
            sp.dma_start(gates[:, 0:2], row_of(io["g_xattn"])).then_inc(gates_loaded, 16)
            sp.dma_start(gates[:, 2:4], row_of(io["g_ffn"])).then_inc(gates_loaded, 16)
            sp.wait_ge(negs_set, 1)
            for slot in scr.rel:
                for t in range(LT):
                    dst = slot[t][:, :, P * (t + 1):P * (t + 2)].rearrange("h p n -> p h n")
                    sp.dma_start(dst, keep.negs[:, :].rearrange("p (h n) -> p h n", n=P))\
                      .then_inc(keep.negs_written, 16)

        @block.scalar
        def _(act):
            act.wait_ge(gates_loaded, 32)
            act.activation(keep.tanh_g[:, :], gates[:, :], ACT.Tanh).then_inc(tanh_ready, 1)


def chunked(w):
    return w.rearrange("(c p) n -> p c n", p=P)


def store_parts(sp, done, target, group, parts):
    for half in range(KC):
        for j in range(2):
            g = group.shift(half * 2 + j).value()
            dst = target[bass.ds(g, 1)].rearrange("o c p t -> p (o c) t")
            sp.dma_start(dst, parts[64 * j:64 * j + 64, half, :, :]).then_inc(done, 16)


STORES = 4


def project_context(nc, io, keep, scr):
    with Phase(nc, "context") as ph:
        rk = ph.sb("rk", [P, KC, D])
        pos = ph.sb("pos", [P, KC, L])
        wk = [ph.sb(f"wk{i}", [P, KC, D]) for i in range(2)]
        wv = ph.sb("wv", [P, KC, 2 * D])
        bk = ph.sb("bk", [P, KC])
        bv = ph.sb("bv", [P, D])
        ctx = [ph.sb(f"ctx{i}", [P, KC, L]) for i in range(2)]
        f = [ph.sb(f"f{i}", [P, KC, L]) for i in range(2)]
        rest = ph.sb("rest", [P, KC, L])
        parts = [ph.sb(f"parts{i}", [P, KC, PARTS, L], BF16) for i in range(2)]
        vx = [[ph.sb(f"vx{i}{s}", [P, H, 32]) for s in range(2)] for i in range(2)]
        mask_i = ph.sb("mask_i", [B, L], I32)
        mask_p = ph.sb("mask_p", [B, 2, L], BF16)
        proj = [ph.ps(f"proj{i}", [P, KC, L]) for i in range(2)]
        vps = [ph.ps(f"v{i}", [P, 2 * D]) for i in range(2)]

        pos_loaded, w_loaded = ph.sem("pos_loaded"), ph.sem("w_loaded")
        ctx_loaded, ctx_read = ph.sems("ctx_loaded", 2), ph.sem("ctx_read")
        proj_ready, proj_free, f_ready = ph.sem("proj_ready"), ph.sem("proj_free"), ph.sem("f_ready")
        rest_ready, part1_ready, split_done = ph.sem("rest_ready"), ph.sem("part1_ready"), ph.sem("split_done")
        parts_out = ph.sems("parts_out", 2)
        ones_set, v_ready, v_copied = ph.sem("ones_set"), ph.sem("v_ready"), ph.sem("v_copied")
        v_out = ph.sems("v_out", 2)
        mask_loaded, mask_ready, mask_out = ph.sem("mask_loaded"), ph.sem("mask_ready"), ph.sem("mask_out")
        block = ph.block()
        V_CREDIT = 3
        CTX_CREDIT = 2

        @block.sync
        def _(sp):
            sp.dma_start(rk[:, :, :], chunked(io["r_kernel"])).then_inc(pos_loaded, 16)
            sp.dma_start(pos[:, :, :], chunked(io["pos_T"][:, 1:L + 1])).then_inc(pos_loaded, 16)
            for i, w in enumerate((io["L0_WkT"], io["L1_WkT"])):
                sp.dma_start(wk[i][:, :, :], chunked(w)).then_inc(w_loaded, 16)
            for i, w in enumerate((io["L0_WvT"], io["L1_WvT"])):
                sp.dma_start(wv[:, :, i * D:(i + 1) * D], chunked(w)).then_inc(w_loaded, 16)
            sp.dma_start(bk[:, :], io["L0_bk"].rearrange("(c p) -> p c", p=P), allow_slow_non_contiguous=True)\
                  .then_inc(w_loaded, 16)
            sp.dma_start(bv[:, :], row_of(io["L0_bv"])).then_inc(w_loaded, 16)
            sp.dma_start(mask_i[:, :], io["mask"]).then_inc(mask_loaded, 16)
            for s in (*parts_out, *v_out):
                sp.sem_inc(s, 1)
            sp.wait_ge(split_done, 1 + 1)
            store_parts(sp, parts_out[0], scr.pe, Count(0), parts[0])
            sp.wait_ge(mask_ready, 2)
            sp.dma_start(scr.mask.rearrange("c b t -> b c t"), mask_p[:, :, :]).then_inc(mask_out, 16)
            for b in batches(sp):
                for i, target in enumerate((scr.k0, scr.k1)):
                    b.wait(sp, split_done, 2, 2 + i + 1)
                    store_parts(sp, parts_out[(1 + i) % 2], target, Count(4 * b.n, b.it, 8), parts[(1 + i) % 2])
                for t in range(LT):
                    b.wait(sp, v_copied, 2 * LT, 2 * (t + 1) + V_CREDIT)
                    for i, target in enumerate((scr.v0, scr.v1)):
                        dst = target[bass.ds(b.value(), 1), :, :, t, :].rearrange("o g p n -> p (o g) n")
                        sp.dma_start(dst, vx[i][t % 2][:, :, :].rearrange("p (g h) d -> p g (h d)", h=HG))\
                          .then_inc(v_out[t % 2], 16)
            sp.wait_ge(mask_out, 16)
            sp.wait_ge(parts_out[0], 16 * STORES * (B + 1) + 1)
            sp.wait_ge(parts_out[1], 16 * STORES * B + 1)
            for s in v_out:
                sp.wait_ge(s, 16 * B * LT + 1)

        @block.gpsimd
        def _(pool):
            for row in vx:
                for t in row:
                    pool.memset(t[:, :, :], 1.0).then_inc(ones_set, 1)
            for b in batches(pool):
                b.wait(pool, ctx_read, 1, 1)
                src = io["ctx_T"].rearrange("(c p) n -> p c n", p=P)[:, :, bass.ds(b.value(L), L)]
                pool.dma_start(ctx[b.slot(2)][:, :, :], src).then_inc(ctx_loaded[b.slot(2)], 16)

        @block.tensor
        def _(pe):
            def operand(slot, w, x):
                for half in range(KC):
                    for c in range(KC):
                        mm = pe.matmul(proj[slot][:, half, :], w[:, c, half * P:(half + 1) * P], x[:, c, :],
                                       start=(c == 0), stop=(c == KC - 1))
                mm.then_inc(proj_ready, 1)

            pe.sem_inc(ctx_read, CTX_CREDIT)
            pe.wait_ge(pos_loaded, 32)
            operand(0, rk, pos)
            pe.wait_ge(w_loaded, 16 * 6)
            for b in batches(pe):
                b.wait_uses(pe, ctx_loaded[b.slot(2)], 2, 16, 16)
                for i in range(2):
                    b.wait(pe, proj_free, 2, i + 1)
                    operand((1 + i) % 2, wk[i], ctx[b.slot(2)])
                for t in range(LT):
                    b.wait(pe, v_copied, 2 * LT, 2 * (t - 1) + V_CREDIT)
                    for c in range(KC):
                        mm = pe.matmul(vps[t % 2][:, :], ctx[b.slot(2)][:, c, t * P:(t + 1) * P], wv[:, c, :],
                                       start=(c == 0), stop=(c == KC - 1))
                    mm.then_inc(v_ready, 1)
                b.wait(pe, v_ready, LT, LT)
                pe.sem_inc(ctx_read, 1)

        @block.scalar
        def _(act):
            def part0(slot, n, bias=(0.0, 0.0)):
                n.wait(act, split_done, 1, -1 + 1)
                n.wait(act, proj_ready, 1, 1)
                for half in range(KC):
                    act.activation(f[slot][:, half, :], proj[slot][:, half, :], ACT.Identity,
                                   bias=bias[half]).then_inc(f_ready, 1)
                for half in range(KC):
                    ins = act.activation(parts[slot][:, half, 2, :], proj[slot][:, half, :], ACT.Identity,
                                         bias=bias[half])
                    ins.then_inc(f_ready if half == 0 else proj_free, 1)

            act.sem_inc(proj_free, 1)
            part0(0, Count(0))
            act.wait_ge(w_loaded, 16 * 6)
            for b in batches(act):
                for i, bias in enumerate(((bk[:, 0:1], bk[:, 1:2]), (0.0, 0.0))):
                    n = Count(1 + i + 2 * b.n, b.it, 4)
                    n.wait_uses(act, parts_out[(1 + i) % 2], 2, 16 * STORES, 1)
                    part0((1 + i) % 2, n, bias)

        @block.vector
        def _(dve):
            def rest_parts(slot, n):
                n.wait(dve, f_ready, 3, 3)
                n.wait(dve, proj_free, 1, 1 + 1)
                n.wait(dve, split_done, 1, 1)
                dve.tensor_tensor(rest[:, :, :], f[slot][:, :, :], parts[slot][:, :, 2, :], ALU.subtract)\
                   .then_inc(rest_ready, 1)
                n.wait(dve, rest_ready, 1, 1)
                dve.tensor_copy(parts[slot][:, :, 1, :], rest[:, :, :]).then_inc(part1_ready, 1)
                n.wait(dve, part1_ready, 1, 1)
                dve.tensor_tensor(parts[slot][:, :, 0, :], rest[:, :, :], parts[slot][:, :, 1, :], ALU.subtract)\
                   .then_inc(split_done, 1)

            dve.sem_inc(split_done, 1)
            dve.sem_inc(v_copied, V_CREDIT)
            rest_parts(0, Count(0))
            dve.wait_ge(mask_loaded, 16)
            dve.tensor_scalar(mask_p[:, 0, :], mask_i[:, :], -9984.0, None, ALU.mult).then_inc(mask_ready, 1)
            dve.tensor_scalar(mask_p[:, 1, :], mask_i[:, :], -16.0, None, ALU.mult).then_inc(mask_ready, 1)
            dve.wait_ge(ones_set, 4)
            dve.wait_ge(w_loaded, 16 * 6)
            for b in batches(dve):
                for i in range(2):
                    rest_parts((1 + i) % 2, Count(1 + i + 2 * b.n, b.it, 4))
                for t in range(LT):
                    b.wait(dve, v_ready, LT, t + 1)
                    Count(LT * b.n + t, b.it, 2 * LT).wait_uses(dve, v_out[t % 2], 2, 32, 1)
                    v = [vps[t % 2][:, i * D:(i + 1) * D].rearrange("p (h d) -> p h d", d=DH) for i in range(2)]
                    dve.tensor_tensor(vx[0][t % 2][:, :, 0:DH], v[0], bv[:, :].rearrange("p (h d) -> p h d", d=DH),
                                      ALU.add).then_inc(v_copied, 1)
                    dve.tensor_copy(vx[1][t % 2][:, :, 0:DH], v[1]).then_inc(v_copied, 1)


def project_queries(nc, io, keep, scr, name, load, wqT, outputs):
    NO = len(outputs)
    with Phase(nc, name) as ph:
        wq = ph.sb("wq", [P, KC, D])
        bias_in = ph.sb("bias_in", [P, NO, 2, KC])
        bias = ph.sb("bias", [P, NO, KC])
        stats = ph.sb("stats", [P, LT, 6])
        mv = ph.sb("mv", [P, LT, 2])
        rstd = ph.sb("rstd", [P, LT])
        half_power = ph.sb("half_power", [P, LT])
        xn = [ph.sb(f"xn{i}", [P, LT, D]) for i in range(2)]
        xT = [ph.sb(f"xT{i}", [P, KC, L]) for i in range(2)]
        f = [ph.sb(f"f{i}", [P, KC, L]) for i in range(2)]
        rest = ph.sb("rest", [P, KC, L])
        parts = [ph.sb(f"parts{i}", [P, KC, PARTS, L], BF16) for i in range(2)]
        turned = [ph.ps(f"turned{c}", [P, L]) for c in range(KC)]
        proj = [ph.ps(f"proj{i}", [P, KC, L]) for i in range(2)]

        x_loaded, w_loaded = ph.sem("x_loaded"), ph.sem("w_loaded")
        bias_ready = ph.sem("bias_ready")
        stats_ready, mv_ready, var_ready, rstd_ready = map(ph.sem, ["stats", "mv", "var", "rstd"])
        power_set, xn_ready, turned_ready, xT_ready = map(ph.sem, ["power_set", "xn", "turned", "xT"])
        proj_ready, f_ready, p0_ready = ph.sem("proj_ready"), ph.sem("f_ready"), ph.sem("p0_ready")
        rest_ready, part1_ready, split_done = ph.sem("rest_ready"), ph.sem("part1_ready"), ph.sem("split_done")
        parts_out = ph.sems("parts_out", 2)
        dve_passed, pool_passed = ph.sem("dve_passed"), ph.sem("pool_passed")
        block = ph.block()
        SPLIT_CREDIT = 2
        P0_CREDIT = NO * KC + 1
        BIASES = [bs for _, _, bs in outputs]
        n_bias = sum(map(len, BIASES))

        @block.sync
        def _(sp):
            if load:
                sp.dma_start(keep.x[:, :].rearrange("p (t d) -> p t d", d=D),
                             io["x"].rearrange("(t p) d -> p t d", p=P)).then_inc(x_loaded, 16)
            sp.dma_start(wq[:, :, :], chunked(wqT)).then_inc(w_loaded, 16)
            for o, bs in enumerate(BIASES):
                for j, v in enumerate(bs):
                    sp.dma_start(bias_in[:, o, j, :], v.rearrange("(c p) -> p c", p=P), allow_slow_non_contiguous=True)\
                  .then_inc(w_loaded, 16)
            for s in parts_out:
                sp.sem_inc(s, 1)
            for b in batches(sp):
                for o, (target, _, _) in enumerate(outputs):
                    n = Count(NO * b.n + o, b.it, 2 * NO)
                    n.wait(sp, split_done, 1, 1 + SPLIT_CREDIT)
                    store_parts(sp, parts_out[n.slot(2)], target, Count(4 * b.n, b.it, 8), parts[n.slot(2)])
            for s in parts_out:
                sp.wait_ge(s, 16 * STORES * NO * B // 2 + 1)

        @block.gpsimd
        def _(pool):
            pool.memset(half_power[:, :], -0.5).then_inc(power_set, 1)
            pool.wait_ge(power_set, 1)
            for b in batches(pool):
                b.wait(pool, mv_ready, LT, LT, pool_passed)
                pool.tensor_scalar(rstd[:, :], mv[:, :, 1], EPS, None, ALU.add).then_inc(var_ready, 1)
                b.wait(pool, var_ready, 1, 1)
                pool.tensor_tensor(rstd[:, :], rstd[:, :], half_power[:, :], ALU.pow).then_inc(rstd_ready, 1)

        @block.tensor
        def _(pe):
            pe.wait_ge(w_loaded, 16 * (1 + n_bias))
            for b in batches(pe):
                b.wait(pe, xT_ready, KC, 1)
                for t in range(LT):
                    b.wait(pe, xn_ready, LT, t + 1)
                    for c in range(KC):
                        mm = pe.transpose(turned[c][:, t * P:(t + 1) * P],
                                          xn[b.slot(2)][:, t, c * P:(c + 1) * P], keep.ident[:, :])
                mm.then_inc(turned_ready, 1)
                b.wait(pe, xT_ready, KC, KC + 1)
                b.wait(pe, p0_ready, NO * KC, -NO * KC + P0_CREDIT)
                for half in range(KC):
                    for c in range(KC):
                        mm = pe.matmul(proj[b.slot(2)][:, half, :], wq[:, c, half * P:(half + 1) * P],
                                       xT[b.slot(2)][:, c, :], start=(c == 0), stop=(c == KC - 1))
                mm.then_inc(proj_ready, 1)

        @block.scalar
        def _(act):
            act.sem_inc(xT_ready, 1)
            act.sem_inc(p0_ready, P0_CREDIT)
            if n_bias:
                act.wait_ge(bias_ready, sum(1 for bs in BIASES if bs))
            for b in batches(act):
                b.wait(act, turned_ready, 1, 1)
                for c in range(KC):
                    act.activation(xT[b.slot(2)][:, c, :], turned[c][:, :], ACT.Copy).then_inc(xT_ready, 1)
                b.wait(act, proj_ready, 1, 1)
                for o, (_, scale, bs) in enumerate(outputs):
                    n = Count(NO * b.n + o, b.it, 2 * NO)
                    n.wait(act, split_done, 1, -1 + SPLIT_CREDIT)
                    n.wait_uses(act, parts_out[n.slot(2)], 2, 16 * STORES, 1)
                    for dst, done in ((f[n.slot(2)][:, :, :], f_ready), (parts[n.slot(2)][:, :, 0, :], p0_ready)):
                        for half in range(KC):
                            act.activation(dst[:, half, :], proj[b.slot(2)][:, half, :], ACT.Identity, scale=scale,
                                           bias=bias[:, o, half:half + 1] if bs else 0.0).then_inc(done, 1)

        @block.vector
        def _(dve):
            dve.sem_inc(split_done, SPLIT_CREDIT)
            if n_bias:
                dve.wait_ge(w_loaded, 16 * (1 + n_bias))
                for o, (_, scale, bs) in enumerate(outputs):
                    if len(bs) == 2:
                        dve.tensor_tensor(bias_in[:, o, 0, :], bias_in[:, o, 0, :], bias_in[:, o, 1, :], ALU.add)\
                           .then_inc(rest_ready, 1)
                        dve.wait_ge(rest_ready, o + 1)
                    dve.tensor_scalar(bias[:, o, :], bias_in[:, o, 0, :], scale, None, ALU.mult).then_inc(bias_ready, 1)
            twos = sum(len(bs) == 2 for bs in BIASES)
            if load:
                dve.wait_ge(x_loaded, 16)
            for b in batches(dve):
                for t in range(LT):
                    xs = keep.x[:, bass.ds(b.value(LT * D, t * D), D)]
                    dve.bn_stats(stats[:, t, :], xs).then_inc(stats_ready, 1)
                for t in range(LT):
                    b.wait(dve, stats_ready, LT, t + 1, dve_passed)
                    dve.bn_aggr(mv[:, t, :], stats[:, t, :]).then_inc(mv_ready, 1)
                b.wait(dve, rstd_ready, 1, 1)
                for t in range(LT):
                    xs = keep.x[:, bass.ds(b.value(LT * D, t * D), D)]
                    dve.tensor_scalar(xn[b.slot(2)][:, t, :], xs, mv[:, t, 0:1], rstd[:, t:t + 1],
                                      ALU.subtract, ALU.mult).then_inc(xn_ready, 1)
                for o in range(NO):
                    n = Count(NO * b.n + o, b.it, 2 * NO)
                    s = n.slot(2)
                    n.wait(dve, f_ready, KC, KC)
                    n.wait(dve, p0_ready, KC, KC + P0_CREDIT)
                    n.wait(dve, split_done, 1, SPLIT_CREDIT)
                    dve.tensor_tensor(rest[:, :, :], f[s][:, :, :], parts[s][:, :, 0, :], ALU.subtract)\
                       .then_inc(rest_ready, 1)
                    n.wait(dve, rest_ready, 1, 1 + twos)
                    dve.tensor_copy(parts[s][:, :, 1, :], rest[:, :, :]).then_inc(part1_ready, 1)
                    n.wait(dve, part1_ready, 1, 1)
                    dve.tensor_tensor(parts[s][:, :, 2, :], rest[:, :, :], parts[s][:, :, 1, :], ALU.subtract)\
                       .then_inc(split_done, 1)


def banks_of(relative):
    if not relative:
        return [[(h, t, 0)] for h in range(HG) for t in range(LT)]
    found = []
    for h in range(0, HG, 2):
        for g in (h, h + 1):
            found += [[(g, 3, 0)], [(g, 2, 0), (g, 0, 3 * P)]]
        found.append([(h, 1, 0), (h + 1, 1, 2 * P)])
    return found


PAIR_PLACE = {3: (0, 2 * L), 2: (L, 2 * L), 0: (L + 3 * P, 2 * L), 1: (4 * L, 2 * P)}
SKEWED = [0, P, 3 * P, 6 * P]
HEAD_COLS = 10 * P


def attention(nc, io, keep, scr, name, q_parts, k_parts, v_cols, relative):
    AHEAD = 1 if relative else 2
    RING = 4
    MASK_ROWS = 0 if relative else 2
    MAX_ROW = SROWS + MASK_ROWS
    K_ALL = MAX_ROW + PARTS
    BANKS = banks_of(relative)
    NB = len(BANKS)
    LOADS = 2 * len(RUNS) + (0 if relative else 1)
    LEAD = 4
    ROUNDS = (NG - 1 - LEAD) // 4
    S_RING = 2 if relative else 4
    REL_RING = 2
    ST_RING = 2
    if relative:
        HALF = NB // 2
        SECOND_AT = FIRST_AT = {i: (2 * i, 2 * i + 2) for i in range(HALF)}
        REL_AT = {i + HALF: banks for i, banks in FIRST_AT.items()}
        VALUES_AT = {HALF + t: t for t in range(LT)}
        TURN_AT = HALF + 2
    else:
        SECOND_AT = FIRST_AT = {i: (i, i + 1) for i in range(NB)}
        REL_AT = {}
        VALUES_AT = {t: t for t in range(LT)}
        TURN_AT = NB // 3
        NORMALISE_AT = {2 * j + 4: j for j in range(4)}
    PIECES = 4

    def width(t):
        return P * (t + 1) if relative else L

    def first_query(mt):
        return P * mt if relative else 0

    PLACE = {}
    for i, bank in enumerate(BANKS):
        for h, t, col in bank:
            PLACE[(h, LT - 1 - t if relative else t)] = (i, col)

    with Phase(nc, name) as ph:
        qst = [ph.sb(f"qst{i}", [P, HG * L], BF16) for i in range(RING)]
        kst = [ph.sb(f"kst{i}", [P, HG * L], BF16) for i in range(RING)]
        vx = [ph.sb(f"vx{i}", [P, LT, HG * 32]) for i in range(2)]
        probs = [ph.sb(f"probs{i}", [P, NB, L]) for i in range(2)]
        mx = [ph.sb(f"mx{i}", [P, LT, HG]) for i in range(2)]
        neg = ph.sb("neg", [P, LT, HG])
        neg_parts = [ph.sb(f"neg_parts{i}", [P, LT, PARTS, HG], BF16) for i in range(2)]
        neg_rows = [ph.sb(f"neg_rows{i}", [PARTS * HG, L], BF16) for i in range(2)]
        sums = ph.sb("sums", [P, L])
        inverse = ph.sb("inverse", [P, L])
        o = [ph.sb(f"o{i}", [P, L]) for i in range(2)]
        s_ps = [ph.ps(f"s{i}", [P, L]) for i in range(S_RING)]
        st_ps = [ph.ps(f"st{i}", [P, L]) for i in range(ST_RING)]
        pv_ps = ph.ps("pv", [P, L])
        turned = ph.ps("turned", [P, 2 * L], BF16)
        if relative:
            qrst = [ph.sb(f"qrst{i}", [SROWS, HG * L], BF16) for i in range(2)]
            pest = ph.sb("pest", [SROWS, H * L], BF16)
            rel = [ph.sb(f"rel{i}", [P, NB // 2 * L]) for i in range(2)]
            skew = [ph.sb(f"skew{i}", [P, HG, HEAD_COLS]) for i in range(2)]
            unused = ph.sb("unused", [P, 2, L], BF16)
            rel_ps = [ph.ps(f"relps{i}", [P, L]) for i in range(REL_RING)]
            qr_loaded = ph.sems("qr_loaded", 2)
            pe_loaded, rel_ready, rel_copied = ph.sem("pe_loaded"), ph.sem("rel_ready"), ph.sem("rel_copied")
            rel_written = ph.sems("rel_written", 4)
            skew_loaded = ph.sems("skew_loaded", 4)

        ones_set = ph.sem("ones_set")
        stack_loaded = ph.sems("stack_loaded", RING)
        rows_loaded = ph.sems("rows_loaded", RING)
        vx_loaded = ph.sems("vx_loaded", 2)
        s_ready, s_reduced = ph.sem("s_ready"), ph.sem("s_reduced")
        neg_ready, neg_part, parts_ready = ph.sem("neg_ready"), ph.sem("neg_part"), ph.sem("parts_ready")
        max_turned, rows_copied = ph.sem("max_turned"), ph.sem("rows_copied")
        st_ready, exp_done = ph.sem("st_ready"), ph.sem("exp_done")
        pv_ready, sums_ready, inverse_ready, o_ready = map(ph.sem, ["pv_ready", "sums", "inverse", "o_ready"])
        o_out = ph.sems("o_out", 2)
        dve_passed, pool_passed, sp_passed = map(ph.sem, ["dve_passed", "pool_passed", "sp_passed"])
        block = ph.block()
        CREDIT = 1

        def within(g):
            return g.it is not None or 0 <= g.n < NG

        def steps(eng, step):
            for n in range(-LEAD, 1):
                step(Count(n))
            with eng.Fori(0, ROUNDS) as it:
                for n in range(1, 5):
                    step(Count(n, it))
            for n in range(4 * ROUNDS + 1, NG + 1):
                step(Count(n))

        def send_maxima(eng, g):
            if within(g):
                g.wait(eng, rows_copied, 1, 1)
                for c in range(PARTS):
                    row = qst[g.slot(RING)][MAX_ROW + c:MAX_ROW + c + 1, :].rearrange("p (h t) -> p h t", h=HG)
                    eng.dma_start(row, neg_rows[g.slot(2)][HG * c:HG * (c + 1), :])\
                       .then_inc(rows_loaded[g.slot(RING)], 16)

        @block.sync
        def _(sp):
            for s in o_out:
                sp.sem_inc(s, CREDIT)
            sp.wait_ge(ones_set, 2 * RING)
            if relative:
                sp.wait_ge(keep.negs_written, 16 * NEG_WRITES)

            def stack(dst, source, g, side, done):
                at = 0
                for run in RUNS:
                    part, count = run[side], run[2]
                    src = source[bass.ds(g.value(), 1), part:part + count]
                    sp.dma_start(dst[at * DH:(at + count) * DH, :],
                                 src.rearrange("o c (d h) t -> (o c d) (h t)", h=HG)).then_inc(done, 16)
                    at += count

            def load_stacks(s):
                g = s.shift(LEAD)
                if within(g):
                    g.wait(sp, st_ready, NB, -3 * NB)
                    stack(qst[g.slot(RING)], q_parts, g, 0, stack_loaded[g.slot(RING)])
                    stack(kst[g.slot(RING)], k_parts, g, 1, stack_loaded[g.slot(RING)])
                    if not relative:
                        b = Count(g.n // 4, g.it, 1)
                        src = scr.mask[:, bass.ds(b.value(), 1), :].rearrange("c b t -> c (b t)")
                        src = bass.AP(src.tensor, src.offset, [list(src.ap[0]), [0, HG], list(src.ap[1])])
                        sp.dma_start(kst[g.slot(RING)][SROWS:SROWS + 2, :].rearrange("c (h t) -> c h t", h=HG), src)\
                          .then_inc(stack_loaded[g.slot(RING)], 16)
                    if relative:
                        g.wait(sp, rel_ready, NB, -NB)
                        stack(qrst[g.slot(2)], scr.qr, g, 0, qr_loaded[g.slot(2)])

            def load_values(s):
                if within(s):
                    s.wait(sp, pv_ready, 1, -1 + CREDIT)
                    src = v_cols[bass.ds(Count(s.n // 4, s.it, 1).value(), 1), s.n % 4]
                    sp.dma_start(vx[s.slot(2)][:, :, :], src.rearrange("o p t n -> (o p) t n"))\
                      .then_inc(vx_loaded[s.slot(2)], 16)

            def write_relative(s):
                g = s.shift(AHEAD + 1)
                if within(g):
                    for pair in range(2):
                        slot = 2 * g.slot(2) + pair
                        g.wait(sp, rel_copied, NB, NB // 2 * (pair + 1))
                        g.wait_uses(sp, skew_loaded[slot], 2, 16 * LT)
                        for t in range(LT):
                            col, head = PAIR_PLACE[t]
                            src = bass.AP(rel[pair][:, :].tensor, rel[pair][:, col:col + 1].offset,
                                          [list(rel[pair][:, :].ap[0]), [head, 2], [1, width(t)]])
                            sp.dma_start(scr.rel[slot][t][:, :, 0:width(t)].rearrange("h p n -> p h n"), src)\
                              .then_inc(rel_written[slot], 16)

            def read_relative(s):
                g = s.shift(AHEAD + 1)
                if within(g):
                    for pair in range(2):
                        slot = 2 * g.slot(2) + pair
                        g.wait_uses(sp, rel_written[slot], 2, 16 * LT, 16 * LT, sp_passed)
                        g.wait(sp, st_ready, NB, -2 * NB + NB // 2 * (pair + 1))
                        for t in range(LT):
                            w = P * (t + 2)
                            src = scr.rel[slot][t]
                            src = bass.AP(src.tensor, src.offset + P - 1, [[w - 1, P], [P * w, 2], [1, width(t)]])
                            dst = skew[g.slot(2)][:, 2 * pair:2 * pair + 2, SKEWED[t]:SKEWED[t] + width(t)]
                            sp.dma_start(dst, src).then_inc(skew_loaded[slot], 16)

            def store(s):
                g = s.shift(-1)
                if within(g):
                    g.wait(sp, o_ready, PIECES, PIECES + CREDIT)
                    sp.dma_start(scr.o[bass.ds(g.value(), 1)].rearrange("o p t -> (o p) t"), o[g.slot(2)][:, :])\
                      .then_inc(o_out[g.slot(2)], 16)

            def step(s):
                if relative:
                    write_relative(s)
                    load_values(s)
                    read_relative(s)
                    load_stacks(s)
                    store(s)
                else:
                    load_values(s)
                    send_maxima(sp, s.shift(1))
                    store(s)
                    load_stacks(s)

            steps(sp, step)
            for s in o_out:
                sp.wait_ge(s, 16 * NG // 2 + CREDIT)
            if relative:
                for s in rel_written:
                    sp.wait_ge(s, 16 * LT * NG // 2)

        @block.gpsimd
        def _(pool):
            for t in (*qst, *kst):
                pool.memset(t[SROWS:P, :], 1.0).then_inc(ones_set, 1)
            pool.wait_ge(ones_set, 2 * RING)

            def step(s):
                g = s.shift(AHEAD)
                if not within(g):
                    return
                to = neg_parts[g.slot(2)]
                g.wait(pool, s_reduced, NB, NB)
                g.wait(pool, max_turned, 1, -1)
                g.wait(pool, parts_ready, 1, 0, pool_passed)
                pool.tensor_scalar(neg[:, :, :], mx[g.slot(2)][:, :, :], -1.0, None, ALU.mult).then_inc(neg_ready, 1)
                g.wait(pool, neg_ready, 2, 1, pool_passed)
                pool.tensor_copy(to[:, :, 0, :], neg[:, :, :]).then_inc(neg_part, 1)
                g.wait(pool, neg_part, 2, 1)
                pool.tensor_tensor(neg[:, :, :], neg[:, :, :], to[:, :, 0, :], ALU.subtract).then_inc(neg_ready, 1)
                g.wait(pool, neg_ready, 2, 2, pool_passed)
                pool.tensor_copy(to[:, :, 1, :], neg[:, :, :]).then_inc(neg_part, 1)
                g.wait(pool, neg_part, 2, 2)
                pool.tensor_tensor(to[:, :, 2, :], neg[:, :, :], to[:, :, 1, :], ALU.subtract).then_inc(parts_ready, 1)

            steps(pool, step)

        @block.tensor
        def _(pe):
            def second(s, first, last):
                q, k = qst[s.slot(RING)], kst[s.slot(RING)]
                for i in range(first, last):
                    if i == 0:
                        s.wait_uses(pe, rows_loaded[s.slot(RING)], RING, 16 * PARTS, 16 * PARTS)
                    if relative and i % (NB // 2) == 0:
                        s.wait_uses(pe, skew_loaded[2 * s.slot(2) + i // (NB // 2)], 2, 16 * LT, 16 * LT)
                    s.wait(pe, exp_done, NB, i - ST_RING + 1)
                    for h, t, col in BANKS[i]:
                        mt = LT - 1 - t if relative else t
                        out = st_ps[i % ST_RING][:, col:col + width(t)]
                        mm = pe.matmul(out, k[0:K_ALL, h * L + mt * P:h * L + (mt + 1) * P],
                                       q[0:K_ALL, h * L + first_query(mt):(h + 1) * L], start=True, stop=True, skip_group_check=relative)
                        for lt in range(mt, LT) if relative else ():
                            part = st_ps[i % ST_RING][:, col + (lt - mt) * P:col + (lt - mt + 1) * P]
                            at = SKEWED[lt] + mt * P
                            mm = pe.matmul(part, skew[s.slot(2)][:, h, at:at + P], keep.ident[:, :], start=False,
                                           stop=True, is_transpose=True, skip_group_check=True)
                    mm.then_inc(st_ready, 1)

            def first_pass(g, first, last):
                q, k = qst[g.slot(RING)], kst[g.slot(RING)]
                for i in range(first, last):
                    if i == 0:
                        g.wait_uses(pe, stack_loaded[g.slot(RING)], RING, 16 * LOADS, 16 * LOADS)
                    g.wait(pe, s_reduced, NB, i - S_RING + 1)
                    for h, t, col in BANKS[i]:
                        mm = pe.matmul(s_ps[i % S_RING][:, col:col + width(t)],
                                       q[0:MAX_ROW, h * L + t * P:h * L + (t + 1) * P],
                                       k[0:MAX_ROW, h * L:h * L + width(t)], start=True, stop=True)
                    mm.then_inc(s_ready, 1)

            def relative_scores(g, first, last):
                for i in range(first, last):
                    if i == 0:
                        g.wait_uses(pe, qr_loaded[g.slot(2)], 2, 16 * len(RUNS), 16 * len(RUNS))
                    g.wait(pe, rel_copied, NB, i - REL_RING + 1)
                    for h, t, col in BANKS[i]:
                        at = ((g.n % 4) * HG + h + 1) * L - width(t)
                        mm = pe.matmul(rel_ps[i % REL_RING][:, col:col + width(t)],
                                       qrst[g.slot(2)][:, h * L + t * P:h * L + (t + 1) * P],
                                       pest[:, at:at + width(t)], start=True, stop=True)
                    mm.then_inc(rel_ready, 1)

            def values(g, first, last):
                if first == 0:
                    g.wait(pe, exp_done, NB, NB)
                    g.wait_uses(pe, vx_loaded[g.slot(2)], 2, 16, 16)
                    g.wait(pe, inverse_ready, PIECES, CREDIT)
                    g.wait(pe, o_ready, PIECES, CREDIT)
                for mt in range(first, last):
                    for h in range(HG):
                        bank, col = PLACE[(h, mt)]
                        w = L - first_query(mt)
                        mm = pe.matmul(pv_ps[32 * h:32 * h + 32, L - w:L], vx[g.slot(2)][:, mt, 32 * h:32 * h + 32],
                                       probs[g.slot(2)][:, bank, col:col + w], start=(mt == 0), stop=(mt == LT - 1),
                                       skip_group_check=True)
                if last == LT:
                    mm.then_inc(pv_ready, 1)

            def turn_maxima(g):
                g.wait(pe, parts_ready, 1, 1)
                g.wait(pe, rows_copied, 1)
                for t in range(LT):
                    mm = pe.transpose(turned[0:PARTS * HG, t * P:(t + 1) * P],
                                      neg_parts[g.slot(2)][:, t, :, :].rearrange("p c h -> p (c h)"),
                                      keep.identb[:, :])
                mm.then_inc(max_turned, 1)

            def step(s):
                for i in range(NB):
                    if i in SECOND_AT and within(s):
                        second(s, *SECOND_AT[i])
                    if i in REL_AT and within(s.shift(AHEAD + 2)):
                        relative_scores(s.shift(AHEAD + 2), *REL_AT[i])
                    if i in FIRST_AT and within(s.shift(AHEAD)):
                        first_pass(s.shift(AHEAD), *FIRST_AT[i])
                    if i in VALUES_AT and within(s.shift(-1)):
                        values(s.shift(-1), VALUES_AT[i], VALUES_AT[i] + 1)
                    if i == TURN_AT and within(s.shift(1)):
                        turn_maxima(s.shift(1))

            pe.sem_inc(pv_ready, CREDIT)
            if relative:
                pe.wait_ge(pe_loaded, 16 * len(RUNS) * (H // HG))
            steps(pe, step)

        @block.scalar
        def _(act):
            def exponentials(s, first, last):
                for i in range(first, last):
                    if i == 0:
                        s.wait(act, pv_ready, 1, -1 + CREDIT)
                    s.wait(act, st_ready, NB, i + 1)
                    act.activation(probs[s.slot(2)][:, i, :], st_ps[i % ST_RING][:, :], ACT.Exp).then_inc(exp_done, 1)

            def copy_relative(g, first, last):
                for n in range(first, last):
                    pair, i = n // (NB // 2), n % (NB // 2)
                    if i == 0:
                        before = g.shift(-1)
                        before.wait_uses(act, rel_written[2 * before.slot(2) + pair], 2, 16 * LT, 16 * LT)
                    g.wait(act, rel_ready, NB, n + 1)
                    w = sum(width(t) for _, t, _ in BANKS[n])
                    act.activation(rel[pair][:, i * L:i * L + w], rel_ps[n % REL_RING][:, 0:w], ACT.Copy)\
                       .then_inc(rel_copied, 1)

            def copy_maxima(g):
                g.wait(act, max_turned, 1, 1)
                old = g.shift(-2)
                old.wait_uses(act, rows_loaded[old.slot(RING)], RING, 16 * PARTS, 16 * PARTS)
                act.activation(neg_rows[g.slot(2)][:, :], turned[0:PARTS * HG, 0:L], ACT.Copy).then_inc(rows_copied, 1)

            def step(s):
                for i in range(NB):
                    if i in SECOND_AT and within(s):
                        exponentials(s, *SECOND_AT[i])
                    if i in REL_AT and within(s.shift(AHEAD + 2)):
                        copy_relative(s.shift(AHEAD + 2), *REL_AT[i])
                    if i == TURN_AT and within(s.shift(1)):
                        copy_maxima(s.shift(1))
                        if relative:
                            send_maxima(act, s.shift(1))

            if relative:
                for hg in range(H // HG):
                    at = 0
                    for _, part, count in RUNS:
                        act.dma_start(pest[at * DH:(at + count) * DH, hg * HG * L:(hg + 1) * HG * L],
                                     scr.pe[hg, part:part + count].rearrange("c (d h) t -> (c d) (h t)", h=HG))\
                          .then_inc(pe_loaded, 16)
                        at += count
            steps(act, step)

        @block.vector
        def _(dve):
            def maxima(g, i):
                if i == 0:
                    g.wait(dve, parts_ready, 1, -1)
                g.wait(dve, s_ready, NB, i + 1)
                if relative and i % (NB // 2) == 0:
                    g.wait_uses(dve, skew_loaded[2 * g.slot(2) + i // (NB // 2)], 2, 16 * LT, 16 * LT)
                if relative:
                    g.wait(dve, s_reduced, NB, i - 1, dve_passed)
                for h, t, col in BANKS[i]:
                    scores, to = s_ps[i % S_RING][:, col:col + width(t)], mx[g.slot(2)][:, t, h:h + 1]
                    if relative:
                        ins = dve.tensor_tensor_reduce(unused[:, i % 2, col:col + width(t)], scores,
                                                       skew[g.slot(2)][:, h, SKEWED[t]:SKEWED[t] + width(t)],
                                                       1.0, LEAST, ALU.add, ALU.max, to)
                    else:
                        ins = dve.tensor_reduce(to, scores, AX.X, ALU.max)
                ins.then_inc(s_reduced, 1)

            def normalise(g, j):
                cols = slice(j * L // PIECES, (j + 1) * L // PIECES)
                if j == 0:
                    g.wait(dve, pv_ready, 1, 1 + CREDIT)
                    g.wait(dve, inverse_ready, PIECES, CREDIT, dve_passed)
                dve.stream_shuffle(sums[:, cols], pv_ps[:, cols], [DH] * 32).then_inc(sums_ready, 1)
                g.wait(dve, sums_ready, PIECES, j + 1)
                if j == 0:
                    g.wait(dve, o_ready, PIECES, CREDIT)
                dve.reciprocal(inverse[:, cols], sums[:, cols]).then_inc(inverse_ready, 1)
                g.wait(dve, inverse_ready, PIECES, j + 1 + CREDIT)
                if j == 0:
                    g.wait_uses(dve, o_out[g.slot(2)], 2, 16, CREDIT)
                dve.tensor_tensor(o[g.slot(2)][:, cols], pv_ps[:, cols], inverse[:, cols], ALU.mult).then_inc(o_ready, 1)

            def step(s):
                for i in range(NB):
                    if not relative and i in NORMALISE_AT and within(s.shift(-1)):
                        normalise(s.shift(-1), NORMALISE_AT[i])
                    if within(s.shift(AHEAD)):
                        maxima(s.shift(AHEAD), i)
                if relative and within(s.shift(-1)):
                    for j in range(PIECES):
                        normalise(s.shift(-1), j)

            dve.sem_inc(inverse_ready, CREDIT)
            dve.sem_inc(o_ready, CREDIT)
            steps(dve, step)


def bcast(ap, dims):
    return bass.AP(ap.tensor, ap.offset, [list(ap.ap[0])] + dims)


class Norm:

    def __init__(self, ph, name):
        self.stats = ph.sb(f"{name}_stats", [P, LT, 6])
        self.mv = ph.sb(f"{name}_mv", [P, LT, 2])
        self.rstd = ph.sb(f"{name}_rstd", [P, LT])
        self.power = ph.sb(f"{name}_power", [P, LT])
        self.stats_ready, self.mv_ready = ph.sem(f"{name}_stats_ready"), ph.sem(f"{name}_mv_ready")
        self.var_ready, self.rstd_ready = ph.sem(f"{name}_var_ready"), ph.sem(f"{name}_rstd_ready")
        self.power_set = ph.sem(f"{name}_power_set")
        self.dve_passed, self.pool_passed = ph.sem(f"{name}_dve_passed"), ph.sem(f"{name}_pool_passed")

    def setup(self, pool):
        pool.memset(self.power[:, :], -0.5).then_inc(self.power_set, 1)
        pool.wait_ge(self.power_set, 1)

    def tile(self, dve, n, t, x):
        dve.bn_stats(self.stats[:, t, :], x).then_inc(self.stats_ready, 1)
        n.wait(dve, self.stats_ready, LT, t + 1, self.dve_passed)
        dve.bn_aggr(self.mv[:, t, :], self.stats[:, t, :]).then_inc(self.mv_ready, 1)

    def invert(self, pool, n):
        n.wait(pool, self.mv_ready, LT, LT, self.pool_passed)
        pool.tensor_scalar(self.rstd[:, :], self.mv[:, :, 1], EPS, None, ALU.add).then_inc(self.var_ready, 1)
        n.wait(pool, self.var_ready, 1, 1)
        pool.tensor_tensor(self.rstd[:, :], self.rstd[:, :], self.power[:, :], ALU.pow).then_inc(self.rstd_ready, 1)

    def apply(self, dve, n, t, out, x):
        if t == 0:
            n.wait(dve, self.rstd_ready, 1, 1)
        return dve.tensor_scalar(out, x, self.mv[:, t, 0:1], self.rstd[:, t:t + 1], ALU.subtract, ALU.mult)


class OutProjection:

    def __init__(self, ph, scr, woT, bo):
        self.scr, self.woT, self.bo = scr, woT, bo
        self.w = ph.sb("op_w", [P, H // HG, D])
        self.o = [ph.sb(f"op_o{i}", [P, H // HG, L]) for i in range(2)]
        self.ps = [ph.ps(f"op_ps{i}", [P, 2, D]) for i in range(2)]
        self.zeroed, self.w_loaded = ph.sem("op_zeroed"), ph.sem("op_w_loaded")
        self.o_loaded, self.ready, self.added = ph.sems("op_o_loaded", 2), ph.sem("op_ready"), ph.sem("op_added")
        self.CREDIT = LT + 1

    def load_weights(self, sp):
        sp.wait_ge(self.zeroed, 1)
        for h in range(H):
            sp.dma_start(self.w[32 * (h % HG):32 * (h % HG) + DH, h // HG, :], self.woT[h * DH:(h + 1) * DH, :])\
              .then_inc(self.w_loaded, 16)
        if self.bo is not None:
            sp.dma_start(self.w[DH:DH + 1, 0, :], row_of(self.bo, 1)).then_inc(self.w_loaded, 16)

    def load(self, sp, b):
        b.wait(sp, self.ready, LT, -LT + self.CREDIT)
        src = self.scr.o[bass.ds(Count(4 * b.n, b.it, 4 * b.per).value(), 4)]
        sp.dma_start(self.o[b.slot(2)][:, :, :], src.rearrange("g p t -> p g t")).then_inc(self.o_loaded[b.slot(2)], 16)

    def multiply(self, pe, b):
        b.wait_uses(pe, self.o_loaded[b.slot(2)], 2, 16, 16)
        for t in range(LT):
            if t % 2 == 0:
                b.wait(pe, self.added, LT, t - 2 + self.CREDIT)
            for g in range(H // HG):
                mm = pe.matmul(self.ps[t // 2][:, t % 2, :], self.o[b.slot(2)][:, g, t * P:(t + 1) * P],
                               self.w[:, g, :], start=(g == 0), stop=(g == H // HG - 1))
            mm.then_inc(self.ready, 1)

    def start_pe(self, pe):
        pe.wait_ge(self.w_loaded, 16 * (H + (self.bo is not None)))
        pe.sem_inc(self.ready, self.CREDIT)

    def add(self, dve, b, t, x, gate):
        b.wait(dve, self.ready, LT, t - t % 2 + 2 + self.CREDIT)
        dve.scalar_tensor_tensor(out=x, in0=self.ps[t // 2][:, t % 2, :], scalar=gate, in1=x, op0=ALU.mult,
                                 op1=ALU.add).then_inc(self.added, 1)


class Gates:

    def __init__(self, ph, gates):
        self.gates = gates
        self.logits = ph.sb("g_logits", [P, NT, E])
        self.most = ph.sb("g_most", [P, NT])
        self.p = ph.sb("g_p", [P, NT, E])
        self.over = ph.sb("g_over", [P, NT, E, E])
        self.over2 = ph.sb("g_over2", [P, NT, E, E])
        self.before = ph.sb("g_before", [P, E, E])
        self.after = ph.sb("g_after", [P, E, E])
        self.masks_set, self.step, self.exp_ready = ph.sem("g_masks"), ph.sem("g_step"), ph.sem("g_exp")
        self.logits_ready = ph.sem("g_logits_ready")

    def setup(self, pool):
        pool.memset(self.before[:, :, :], 1.0).then_inc(self.masks_set, 1)
        pool.memset(self.after[:, :, :], 1.0).then_inc(self.masks_set, 1)
        pool.wait_ge(self.masks_set, 2)
        pool.affine_select(out=self.before[:, :, :], in_=self.before[:, :, :], compare_op=ALU.is_gt, fill=0.0, base=0,
                           pattern=[[1, E], [-1, E]], channel_multiplier=0).then_inc(self.masks_set, 1)
        pool.affine_select(out=self.after[:, :, :], in_=self.after[:, :, :], compare_op=ALU.is_gt, fill=0.0, base=0,
                           pattern=[[-1, E], [1, E]], channel_multiplier=0).then_inc(self.masks_set, 1)

    def exponentiate(self, act):
        act.wait_ge(self.step, 2)
        act.activation(self.p[:, :, :], self.p[:, :, :], ACT.Exp).then_inc(self.exp_ready, 1)

    def compute(self, dve, logits_count, factor):
        done = [0]

        def then(ins):
            done[0] += 1
            ins.then_inc(self.step, 1)
            dve.wait_ge(self.step, done[0])

        per_e, per_tile = [[E, NT], [1, E]], [[1, NT], [0, E]]
        pj = bcast(self.p[:, :, :], [[E, NT], [0, E], [1, E]])
        pe = bcast(self.p[:, :, :], [[E, NT], [1, E], [0, E]])
        before, after = (bcast(m[:, :, :], [[0, NT], [E, E], [1, E]]) for m in (self.before, self.after))
        dve.wait_ge(self.logits_ready, logits_count)
        dve.wait_ge(self.masks_set, 4)
        then(dve.tensor_reduce(self.most[:, :], self.logits[:, :, :], AX.X, ALU.max))
        then(dve.tensor_tensor(self.p[:, :, :], self.logits[:, :, :], bcast(self.most[:, :], per_tile), ALU.subtract))
        dve.wait_ge(self.exp_ready, 1)
        then(dve.tensor_reduce(self.most[:, :], self.p[:, :, :], AX.X, ALU.add))
        then(dve.reciprocal(self.most[:, :], self.most[:, :]))
        then(dve.tensor_tensor(self.p[:, :, :], self.p[:, :, :], bcast(self.most[:, :], per_tile), ALU.mult))
        then(dve.tensor_tensor(self.over[:, :, :, :], pj, pe, ALU.is_gt))
        then(dve.tensor_tensor(self.over[:, :, :, :], self.over[:, :, :, :], after, ALU.mult))
        then(dve.tensor_tensor(self.over2[:, :, :, :], pj, pe, ALU.is_ge))
        then(dve.tensor_tensor(self.over2[:, :, :, :], self.over2[:, :, :, :], before, ALU.mult))
        then(dve.tensor_tensor(self.over[:, :, :, :], self.over[:, :, :, :], self.over2[:, :, :, :], ALU.add))
        then(dve.tensor_reduce(self.logits[:, :, :], self.over[:, :, :, :], AX.X, ALU.add))
        then(dve.tensor_scalar(self.logits[:, :, :], self.logits[:, :, :], TOP - 0.5, factor, ALU.is_lt, ALU.mult))
        then(dve.tensor_tensor(self.gates[:, :, :], self.logits[:, :, :], self.p[:, :, :], ALU.mult))


def first_mixture(nc, io, keep, scr):
    with Phase(nc, "mix0") as outer:
        ww = outer.sb("ww", [P, KC, E * D])
        gates = outer.sb("gates", [P, NT, E])

        with Phase(nc, "prep0") as ph:
            wi = ph.sb("wi", [P, E, KC, D])
            wo = ph.sb("wo", [P, E, KC, D])
            wr = ph.sb("wr", [P, KC, E])
            xn = [ph.sb(f"xn{i}", [P, LT, D]) for i in range(2)]
            xT = [ph.sb(f"xT{i}", [P, LT, KC, P]) for i in range(2)]
            norm, project, gating = Norm(ph, "norm"), OutProjection(ph, scr, io["L0_WoT"], io["L0_bo"]), Gates(ph, gates)
            ww_ps = [ph.ps(f"ww_ps{i}", [P, D]) for i in range(2)]
            turned = [ph.ps(f"turned{c}", [P, L]) for c in range(KC)]
            logits_ps = ph.ps("logits_ps", [P, LT, E])
            w_loaded, ww_ready, ww_copied = ph.sem("w_loaded"), ph.sem("ww_ready"), ph.sem("ww_copied")
            xn_ready, turned_ready, xT_ready = ph.sem("xn_ready"), ph.sem("turned_ready"), ph.sem("xT_ready")
            logits_done = ph.sem("logits_done")
            xT_out = ph.sems("xT_out", 2)
            block = ph.block()
            X_CREDIT = L_CREDIT = 1

            @block.sync
            def _(sp):
                for s in xT_out:
                    sp.sem_inc(s, 1)
                sp.dma_start(wi[:, :, :, :].rearrange("p e c n -> p (e c) n"), io["L0_WiT"].rearrange("e (c p) n -> p (e c) n", p=P)).then_inc(w_loaded, 16)
                sp.dma_start(wo[:, :, :, :].rearrange("p e c n -> p (e c) n"), io["L0_Wo"].rearrange("e (c p) n -> p (e c) n", p=P)).then_inc(w_loaded, 16)
                sp.dma_start(wr[:, :, :], chunked(io["L0_Wr"])).then_inc(w_loaded, 16)
                project.load_weights(sp)
                for b in batches(sp):
                    project.load(sp, b)
                for s in xT_out:
                    sp.wait_ge(s, 16 * B // 2 + 1)

            @block.gpsimd
            def _(pool):
                pool.memset(project.w[:, :, :], 0.0).then_inc(project.zeroed, 1)
                pool.wait_ge(project.zeroed, 1)
                norm.setup(pool)
                gating.setup(pool)
                for b in batches(pool):
                    norm.invert(pool, b)

            @block.tensor
            def _(pe):
                pe.wait_ge(w_loaded, 16 * 3)
                for n in range(KC * E):
                    half, e = n % KC, n // KC
                    if n >= 2:
                        pe.wait_ge(ww_copied, n - 1)
                    for c in range(KC):
                        mm = pe.matmul(ww_ps[n % 2][:, :], wi[:, e, c, half * P:(half + 1) * P], wo[:, e, c, :],
                                       start=(c == 0), stop=(c == KC - 1))
                    mm.then_inc(ww_ready, 1)
                project.start_pe(pe)
                for b in batches(pe):
                    project.multiply(pe, b)
                    b.wait(pe, xT_ready, KC, X_CREDIT)
                    for t in range(LT):
                        b.wait(pe, xn_ready, LT, t + 1)
                        for c in range(KC):
                            mm = pe.transpose(turned[c][:, t * P:(t + 1) * P], xn[b.slot(2)][:, t, c * P:(c + 1) * P],
                                              keep.ident[:, :])
                    mm.then_inc(turned_ready, 1)
                    b.wait(pe, xT_ready, KC, KC + X_CREDIT)
                    b.wait(pe, gating.logits_ready, 1, L_CREDIT)
                    for t in range(LT):
                        for c in range(KC):
                            mm = pe.matmul(logits_ps[:, t, :], xT[b.slot(2)][:, t, c, :], wr[:, c, :],
                                           start=(c == 0), stop=(c == KC - 1))
                    mm.then_inc(logits_done, 1)

            @block.scalar
            def _(act):
                act.sem_inc(xT_ready, X_CREDIT)
                act.sem_inc(gating.logits_ready, L_CREDIT)
                for b in batches(act):
                    s = b.slot(2)
                    b.wait(act, turned_ready, 1, 1)
                    b.wait_uses(act, xT_out[s], 2, 16, 1)
                    for c in range(KC):
                        act.activation(xT[s][:, :, c, :], turned[c][:, :].rearrange("p (t n) -> p t n", n=P), ACT.Copy)\
                           .then_inc(xT_ready, 1)
                    b.wait(act, xT_ready, KC, KC + X_CREDIT)
                    act.dma_start(scr.xT[bass.ds(b.value(LT), LT)].rearrange("t p n -> p t n"),
                                  xT[s][:, :, :, :].rearrange("p t c n -> p t (c n)")).then_inc(xT_out[s], 16)
                    b.wait(act, logits_done, 1, 1)
                    to = gating.logits[:, bass.ds(b.value(LT), LT), :]
                    act.activation(to, logits_ps[:, :, :], ACT.Copy).then_inc(gating.logits_ready, 1)
                gating.exponentiate(act)

            @block.vector
            def _(dve):
                for n in range(KC * E):
                    half, e = n % KC, n // KC
                    dve.wait_ge(ww_ready, n + 1)
                    dve.tensor_copy(ww[:, half, e * D:(e + 1) * D], ww_ps[n % 2][:, :]).then_inc(ww_copied, 1)
                dve.sem_inc(project.added, project.CREDIT)
                for b in batches(dve):
                    tiles = [keep.x[:, bass.ds(b.value(LT * D, t * D), D)] for t in range(LT)]
                    for t in range(LT):
                        project.add(dve, b, t, tiles[t], keep.tanh_g[:, 0:1])
                        b.wait(dve, project.added, LT, t + 1 + project.CREDIT, norm.dve_passed)
                        norm.tile(dve, b, t, tiles[t])
                    for t in range(LT):
                        norm.apply(dve, b, t, xn[b.slot(2)][:, t, :], tiles[t]).then_inc(xn_ready, 1)
                gating.compute(dve, B + L_CREDIT, keep.tanh_g[:, 2:3])

        with Phase(nc, "run0") as ph:
            CH = E * D // L
            xT = [ph.sb(f"xT{i}", [P, KC, P]) for i in range(2)]
            y_ps = [ph.ps(f"y{i}", [P, L]) for i in range(CH)]
            xT_loaded, y_ready, added = ph.sems("xT_loaded", 2), ph.sem("y_ready"), ph.sem("added")
            block = ph.block()
            Y_CREDIT = CH + 1

            def tiles(eng):
                with eng.Fori(0, NT // 2) as it:
                    for par in range(2):
                        yield Count(par, it, per=2)

            @block.sync
            def _(sp):
                for t in tiles(sp):
                    t.wait(sp, y_ready, CH, -CH + Y_CREDIT)
                    sp.dma_start(xT[t.slot(2)][:, :, :],
                                 scr.xT[bass.ds(t.value(), 1)].rearrange("o p (c n) -> (o p) c n", n=P))\
                      .then_inc(xT_loaded[t.slot(2)], 16)

            @block.tensor
            def _(pe):
                pe.sem_inc(y_ready, Y_CREDIT)
                for t in tiles(pe):
                    t.wait_uses(pe, xT_loaded[t.slot(2)], 2, 16, 16)
                    for ch in range(CH):
                        t.wait(pe, added, E, 2 * (ch - CH + 1) + 2 * CH)
                        for c in range(KC):
                            mm = pe.matmul(y_ps[ch][:, :], xT[t.slot(2)][:, c, :], ww[:, c, ch * L:(ch + 1) * L],
                                           start=(c == 0), stop=(c == KC - 1))
                        mm.then_inc(y_ready, 1)

            @block.vector
            def _(dve):
                dve.sem_inc(added, 2 * CH)
                for t in tiles(dve):
                    x = keep.x[:, bass.ds(t.value(D), D)]
                    for e in range(E):
                        t.wait(dve, y_ready, CH, e // 2 + 1 + Y_CREDIT)
                        t.wait(dve, added, E, e + 2 * CH)
                        gate = gates[:, bass.ds(t.value(), 1), e:e + 1].rearrange("p o e -> p (o e)")
                        dve.scalar_tensor_tensor(out=x, in0=y_ps[e // 2][:, (e % 2) * D:(e % 2 + 1) * D], scalar=gate,
                                                 in1=x, op0=ALU.mult, op1=ALU.add).then_inc(added, 1)


class TileNorm:

    RING = 4

    def __init__(self, ph, name):
        self.stats = ph.sb(f"{name}_stats", [P, self.RING, 6])
        self.mv = ph.sb(f"{name}_mv", [P, self.RING, 2])
        self.rstd = ph.sb(f"{name}_rstd", [P, self.RING])
        self.power = ph.sb(f"{name}_power", [P, 1])
        self.stats_ready, self.mv_ready = ph.sem(f"{name}_stats_ready"), ph.sem(f"{name}_mv_ready")
        self.var_ready, self.rstd_ready = ph.sem(f"{name}_var_ready"), ph.sem(f"{name}_rstd_ready")
        self.power_set, self.applied = ph.sem(f"{name}_power_set"), ph.sem(f"{name}_applied")
        self.dve_passed, self.pool_passed = ph.sem(f"{name}_dve_passed"), ph.sem(f"{name}_pool_passed")

    def setup(self, pool):
        pool.memset(self.power[:, :], -0.5).then_inc(self.power_set, 1)
        pool.wait_ge(self.power_set, 1)

    def tile(self, dve, n, x):
        s = n.slot(self.RING)
        n.wait(dve, self.applied, 1, 1 - self.RING, self.dve_passed)
        dve.bn_stats(self.stats[:, s, :], x).then_inc(self.stats_ready, 1)
        n.wait(dve, self.stats_ready, 1, 1, self.dve_passed)
        dve.bn_aggr(self.mv[:, s, :], self.stats[:, s, :]).then_inc(self.mv_ready, 1)

    def invert(self, pool, n):
        s = n.slot(self.RING)
        n.wait(pool, self.mv_ready, 1, 1, self.pool_passed)
        pool.tensor_scalar(self.rstd[:, s:s + 1], self.mv[:, s, 1:2], EPS, None, ALU.add).then_inc(self.var_ready, 1)
        n.wait(pool, self.var_ready, 1, 1)
        pool.tensor_tensor(self.rstd[:, s:s + 1], self.rstd[:, s:s + 1], self.power[:, :], ALU.pow)\
            .then_inc(self.rstd_ready, 1)

    def apply(self, dve, n, out, x):
        s = n.slot(self.RING)
        n.wait(dve, self.rstd_ready, 1, 1)
        dve.tensor_scalar(out, x, self.mv[:, s, 0:1], self.rstd[:, s:s + 1], ALU.subtract, ALU.mult)\
           .then_inc(self.applied, 1)


def staged(eng, step, total, unroll, lag):
    peeled = unroll * (2 if lag > 1 else 1)
    for n in range(peeled):
        step(Count(n))
    with eng.Fori(0, (total - peeled) // unroll) as it:
        for n in range(peeled, peeled + unroll):
            step(Count(n, it, unroll))
    for n in range(total, total + lag):
        step(Count(n))


def second_mixture(nc, io, keep, scr, out):
    with Phase(nc, "mix1") as outer:
        w1 = outer.sb("w1", [P, E, KC, F])
        w2 = outer.sb("w2", [P, E, F // P, D])
        xp = outer.sb("xp", [P, NT * D])
        hT = outer.sb("hT", [P, KC, NT * P])
        gates = outer.sb("gates", [P, NT, E])
        experts_loaded = outer.sem("experts_loaded")
        with Phase(nc, "qkv") as middle:
            qkv = middle.sb("qkv", [P, NT * 3 * D])
            project_block(nc, io, keep, scr, xp, qkv, w1, w2, experts_loaded)
            attend_batches(nc, io, keep, xp, qkv, hT, gates)
        mix_experts(nc, keep, out, xp, hT, gates, w1, w2, experts_loaded)


def project_block(nc, io, keep, scr, xp, qkv, w1, w2, experts_loaded):
    TWO = 2
    O_RING = 4
    LAG = 4
    with Phase(nc, "block") as ph:
        wo = ph.sb("wo", [P, H // HG, D])
        o = [ph.sb(f"o{i}", [P, H // HG, P]) for i in range(O_RING)]
        win = ph.sb("win", [P, KC, 3 * D])
        b_in = ph.sb("b_in", [P, 3 * D])
        ln = ph.sb("ln", [P, 2, KC])
        hn = [ph.sb(f"hn{i}", [P, D]) for i in range(TWO)]
        hnT = [ph.sb(f"hnT{i}", [P, KC, P]) for i in range(TWO)]
        norm_a, norm_b = TileNorm(ph, "norm_a"), TileNorm(ph, "norm_b")
        o_ps = [ph.ps(f"o_ps{i}", [P, D]) for i in range(TWO)]
        turned = [ph.ps(f"turned{i}", [P, KC, P]) for i in range(TWO)]
        qk_ps = [ph.ps(f"qk_ps{i}", [P, 2 * D]) for i in range(TWO)]
        v_ps = [ph.ps(f"v_ps{i}", [P, D]) for i in range(TWO)]
        zeroed, w_loaded = ph.sem("zeroed"), ph.sem("w_loaded")
        o_loaded = ph.sems("o_loaded", O_RING)
        o_ready, added, turned_ready, hnT_ready = map(ph.sem, ["o_ready", "added", "turned_ready", "hnT_ready"])
        qkv_ready, qkv_copied = ph.sem("qkv_ready"), ph.sem("qkv_copied")
        block = ph.block()
        WEIGHTS = H + 4

        def within(u):
            return u.it is not None or 0 <= u.n < NT

        @block.sync
        def _(sp):
            sp.wait_ge(zeroed, 1)
            for h in range(H):
                sp.dma_start(wo[32 * (h % HG):32 * (h % HG) + DH, h // HG, :], io["L1_WoT"][h * DH:(h + 1) * DH, :])\
                  .then_inc(w_loaded, 16)

            def step(u):
                if not within(u):
                    return
                u.wait(sp, o_ready, 1, 1 - O_RING)
                batch, t = Count(4 * (u.n // LT), u.it, 4), u.n % LT
                src = scr.o[bass.ds(batch.value(), H // HG), :, t * P:(t + 1) * P]
                sp.dma_start(o[u.slot(O_RING)][:, :, :], src.rearrange("g p t -> p g t"))\
                  .then_inc(o_loaded[u.slot(O_RING)], 16)

            staged(sp, step, NT, 4, LAG)
            for e in range(E):
                sp.dma_start(w1[:, e, :, :], chunked(io["w1"][e])).then_inc(experts_loaded, 16)
                sp.dma_start(w2[:, e, :, :], chunked(io["w2"][e])).then_inc(experts_loaded, 16)

        @block.gpsimd
        def _(pool):
            pool.memset(wo[:, :, :], 0.0).then_inc(zeroed, 1)
            norm_a.setup(pool)
            norm_b.setup(pool)

            def step(u):
                if within(u):
                    norm_a.invert(pool, u)
                if within(u.shift(-1)):
                    norm_b.invert(pool, u.shift(-1))

            staged(pool, step, NT, 4, LAG)

        @block.tensor
        def _(pe):
            pe.wait_ge(w_loaded, 16 * WEIGHTS)

            def step(u):
                if within(u):
                    u.wait_uses(pe, o_loaded[u.slot(O_RING)], O_RING, 16, 16)
                    u.wait(pe, added, 1, -1)
                    for g in range(H // HG):
                        mm = pe.matmul(o_ps[u.slot(2)][:, :], o[u.slot(O_RING)][:, g, :], wo[:, g, :],
                                       start=(g == 0), stop=(g == H // HG - 1))
                    mm.then_inc(o_ready, 1)
                m = u.shift(-3)
                if within(m):
                    m.wait(pe, norm_b.applied, 1, 1)
                    m.wait(pe, hnT_ready, KC, -KC)
                    for c in range(KC):
                        mm = pe.transpose(turned[m.slot(2)][:, c, :], hn[m.slot(2)][:, c * P:(c + 1) * P], keep.ident[:, :])
                    mm.then_inc(turned_ready, 1)
                m = u.shift(-4)
                if within(m):
                    m.wait(pe, hnT_ready, KC, KC)
                    m.wait(pe, qkv_copied, 2, -2)
                    for to, cols in ((qk_ps, slice(0, 2 * D)), (v_ps, slice(2 * D, 3 * D))):
                        for c in range(KC):
                            mm = pe.matmul(to[m.slot(2)][:, :], hnT[m.slot(2)][:, c, :], win[:, c, cols],
                                           start=(c == 0), stop=(c == KC - 1))
                    mm.then_inc(qkv_ready, 1)

            staged(pe, step, NT, 4, LAG)

        @block.scalar
        def _(act):
            act.dma_start(win[:, :, :], chunked(io["in_WT"])).then_inc(w_loaded, 16)
            act.dma_start(b_in[:, :], row_of(io["in_b"])).then_inc(w_loaded, 16)
            for i, v in enumerate((io["ln1_w"], io["ln1_b"])):
                act.dma_start(ln[:, i, :], v.rearrange("(c p) -> p c", p=P), allow_slow_non_contiguous=True)\
                   .then_inc(w_loaded, 16)
            act.wait_ge(w_loaded, 16 * WEIGHTS)

            def step(u):
                m = u.shift(-3)
                if within(m):
                    m.wait(act, turned_ready, 1, 1)
                    m.wait(act, qkv_ready, 1, -1)
                    for c in range(KC):
                        act.activation(hnT[m.slot(2)][:, c, :], turned[m.slot(2)][:, c, :], ACT.Identity,
                                       scale=ln[:, 0, c:c + 1], bias=ln[:, 1, c:c + 1]).then_inc(hnT_ready, 1)

            staged(act, step, NT, 4, LAG)

        @block.vector
        def _(dve):
            dve.wait_ge(w_loaded, 16 * WEIGHTS)

            def step(u):
                if within(u):
                    x = keep.x[:, bass.ds(u.value(D), D)]
                    u.wait(dve, o_ready, 1, 1)
                    dve.scalar_tensor_tensor(out=x, in0=o_ps[u.slot(2)][:, :], scalar=keep.tanh_g[:, 1:2], in1=x,
                                             op0=ALU.mult, op1=ALU.add).then_inc(added, 1)
                    u.wait(dve, added, 1, 1)
                    norm_a.tile(dve, u, x)
                m = u.shift(-1)
                if within(m):
                    to = xp[:, bass.ds(m.value(D), D)]
                    norm_a.apply(dve, m, to, keep.x[:, bass.ds(m.value(D), D)])
                    m.wait(dve, norm_a.applied, 1, 1)
                    norm_b.tile(dve, m, to)
                m = u.shift(-2)
                if within(m):
                    m.wait(dve, turned_ready, 1, -1)
                    norm_b.apply(dve, m, hn[m.slot(2)][:, :], xp[:, bass.ds(m.value(D), D)])
                m = u.shift(-4)
                if within(m):
                    m.wait(dve, qkv_ready, 1, 1)
                    for ps, at, w in ((qk_ps, 0, 2 * D), (v_ps, 2 * D, D)):
                        dve.tensor_tensor(qkv[:, bass.ds(m.value(3 * D, at), w)], ps[m.slot(2)][:, :],
                                          b_in[:, at:at + w], ALU.add).then_inc(qkv_copied, 1)

            staged(dve, step, NT, 4, LAG)


def attend_batches(nc, io, keep, xp, qkv, hT, gates):
    TWO = 2
    LAG = 4
    ROW = B * H * B
    with Phase(nc, "batches") as ph:
        wout = ph.sb("wout", [P, KC, D])
        b_out = ph.sb("b_out", [P, D])
        ln = ph.sb("ln", [P, 2, KC])
        wr = ph.sb("wr", [P, KC, E])
        products = [ph.sb(f"products{i}", [P, B, D]) for i in range(TWO)]
        scores = ph.sb("scores", [P, LT * ROW])
        probs = ph.sb("probs", [P, LT * ROW])
        most = ph.sb("most", [P, LT * ROW // B])
        attn = [ph.sb(f"attn{i}", [P, D]) for i in range(TWO)]
        attnT = [ph.sb(f"attnT{i}", [P, KC, P]) for i in range(TWO)]
        hn = [ph.sb(f"hn{i}", [P, D]) for i in range(TWO)]
        hnT = [ph.sb(f"hnT{i}", [P, KC, P]) for i in range(TWO)]
        norm, gating = TileNorm(ph, "norm"), Gates(ph, gates)
        turned_a = [ph.ps(f"turned_a{i}", [P, KC * P]) for i in range(TWO)]
        out_ps = [ph.ps(f"out_ps{i}", [P, D]) for i in range(TWO)]
        turned_h = [ph.ps(f"turned_h{i}", [P, KC, P]) for i in range(TWO)]
        logits_ps = [ph.ps(f"logits_ps{i}", [P, E]) for i in range(TWO)]
        w_loaded, masked, bias_added = ph.sem("w_loaded"), ph.sem("masked"), ph.sem("bias_added")
        product_ready, score_ready, soft, exp_ready = map(ph.sem, ["product", "score", "soft", "exp"])
        weighed, attn_ready, a_turned, attnT_ready = map(ph.sem, ["weighed", "attn_ready", "a_turned", "attnT_ready"])
        out_ready, added, h_turned, hnT_ready = map(ph.sem, ["out_ready", "added", "h_turned", "hnT_ready"])
        logits_done, hT_copied, pool_passed = ph.sem("logits_done"), ph.sem("hT_copied"), ph.sem("pool_passed")
        block = ph.block()
        WEIGHTS = 5
        CREDIT = 2

        def within(u):
            return u.it is not None or 0 <= u.n < NT

        def tile(u):
            return Count(LT * (u.n % B) + u.n // B, u.it, 1)

        def rows(u, k, b):
            first = Count(u.n // B, u.it, 1)
            return bcast(qkv[:, bass.ds(first.value(3 * D, k * D), D)], [[LT * 3 * D, b + 1], [1, D]])

        @block.sync
        def _(sp):
            sp.dma_start(wout[:, :, :], chunked(io["out_WT"])).then_inc(w_loaded, 16)
            sp.dma_start(b_out[:, :], row_of(io["out_b"])).then_inc(w_loaded, 16)
            sp.dma_start(wr[:, :, :], chunked(io["router_T"])).then_inc(w_loaded, 16)
            for i, v in enumerate((io["ln2_w"], io["ln2_b"])):
                sp.dma_start(ln[:, i, :], v.rearrange("(c p) -> p c", p=P), allow_slow_non_contiguous=True)\
                  .then_inc(w_loaded, 16)

        @block.gpsimd
        def _(pool):
            pool.memset(scores[:, :], -1.0e30).then_inc(masked, 1)
            norm.setup(pool)
            gating.setup(pool)
            pool.wait_ge(w_loaded, 16 * WEIGHTS)
            with pool.Fori(0, B) as it:
                for t in range(LT):
                    x = xp[:, bass.ds(Count(t, it, LT).value(D), D)]
                    pool.tensor_tensor(x, x, b_out[:, :], ALU.add).then_inc(bias_added, 1)

            def step(u):
                if within(u.shift(-2)):
                    norm.invert(pool, u.shift(-2))
                m = u.shift(-3)
                if within(m):
                    m.wait(pool, hnT_ready, KC, KC, pool_passed)
                    pool.tensor_copy(hT[:, :, bass.ds(tile(m).value(P), P)], hnT[m.slot(2)][:, :, :])\
                        .then_inc(hT_copied, 1)

            staged(pool, step, NT, 4, LAG)

        @block.tensor
        def _(pe):
            pe.wait_ge(w_loaded, 16 * WEIGHTS)

            def step(u):
                if within(u):
                    u.wait(pe, attn_ready, 1, 1)
                    u.wait(pe, attnT_ready, 1, -1)
                    for c in range(KC):
                        mm = pe.transpose(turned_a[u.slot(2)][:, c * P:(c + 1) * P], attn[u.slot(2)][:, c * P:(c + 1) * P],
                                          keep.ident[:, :])
                    mm.then_inc(a_turned, 1)
                m = u.shift(-1)
                if within(m):
                    m.wait(pe, attnT_ready, 1, 1)
                    m.wait(pe, added, 1, -1)
                    for c in range(KC):
                        mm = pe.matmul(out_ps[m.slot(2)][:, :], attnT[m.slot(2)][:, c, :], wout[:, c, :],
                                       start=(c == 0), stop=(c == KC - 1))
                    mm.then_inc(out_ready, 1)
                m = u.shift(-3)
                if within(m):
                    m.wait(pe, norm.applied, 1, 1)
                    m.wait(pe, hnT_ready, KC, -KC)
                    for c in range(KC):
                        mm = pe.transpose(turned_h[m.slot(2)][:, c, :], hn[m.slot(2)][:, c * P:(c + 1) * P], keep.ident[:, :])
                    mm.then_inc(h_turned, 1)
                m = u.shift(-4)
                if within(m):
                    m.wait(pe, hnT_ready, KC, KC)
                    m.wait(pe, gating.logits_ready, 1, -1)
                    for c in range(KC):
                        mm = pe.matmul(logits_ps[m.slot(2)][:, :], hnT[m.slot(2)][:, c, :], wr[:, c, :],
                                       start=(c == 0), stop=(c == KC - 1))
                    mm.then_inc(logits_done, 1)

            staged(pe, step, NT, 4, LAG)

        @block.scalar
        def _(act):
            act.wait_ge(soft, 2)
            act.activation(probs[:, :], probs[:, :], ACT.Exp, scale=DH ** -0.5).then_inc(exp_ready, 1)
            act.wait_ge(w_loaded, 16 * WEIGHTS)

            def step(u):
                if within(u):
                    u.wait(act, a_turned, 1, 1)
                    u.wait(act, out_ready, 1, -1)
                    act.activation(attnT[u.slot(2)][:, :, :].rearrange("p c n -> p (c n)"), turned_a[u.slot(2)][:, :],
                                   ACT.Copy).then_inc(attnT_ready, 1)
                m = u.shift(-3)
                if within(m):
                    m.wait(act, h_turned, 1, 1)
                    m.wait(act, logits_done, 1, -1)
                    m.wait(act, hT_copied, 1, -1)
                    for c in range(KC):
                        act.activation(hnT[m.slot(2)][:, c, :], turned_h[m.slot(2)][:, c, :], ACT.Identity,
                                       scale=ln[:, 0, c:c + 1], bias=ln[:, 1, c:c + 1]).then_inc(hnT_ready, 1)
                m = u.shift(-4)
                if within(m):
                    m.wait(act, logits_done, 1, 1)
                    to = gating.logits[:, bass.ds(tile(m).value(), 1), :].rearrange("p o e -> p (o e)")
                    act.activation(to, logits_ps[m.slot(2)][:, :], ACT.Copy).then_inc(gating.logits_ready, 1)

            staged(act, step, NT, 4, LAG)
            gating.exponentiate(act)

        @block.vector
        def _(dve):
            dve.sem_inc(score_ready, CREDIT)
            dve.wait_ge(masked, 1)
            with dve.Fori(0, LT) as it:
                for b in range(B):
                    u = Count(b, it, B)
                    u.wait(dve, score_ready, 1, -1 + CREDIT)
                    q = bcast(qkv[:, bass.ds(tile(u).value(3 * D), D)], [[0, b + 1], [1, D]])
                    dve.tensor_tensor(products[u.slot(2)][:, 0:b + 1, :], q, rows(u, 1, b), ALU.mult)\
                       .then_inc(product_ready, 1)
                    u.wait(dve, product_ready, 1, 1)
                    to = bcast(scores[:, bass.ds(Count(0, it, 1).value(ROW, b * H * B), H * B)], [[1, b + 1], [B, H]])
                    dve.tensor_reduce(to, products[u.slot(2)][:, 0:b + 1, :].rearrange("p b (h d) -> p b h d", d=DH),
                                      AX.X, ALU.add).then_inc(score_ready, 1)
            dve.wait_ge(score_ready, NT + CREDIT)
            by_head = scores[:, :].rearrange("p (n b) -> p n b", b=B)
            probs_by_head = probs[:, :].rearrange("p (n b) -> p n b", b=B)
            over_keys = bcast(most[:, :], [[1, LT * ROW // B], [0, B]])
            dve.tensor_reduce(most[:, :], by_head, AX.X, ALU.max).then_inc(soft, 1)
            dve.wait_ge(soft, 1)
            dve.tensor_tensor(probs_by_head, by_head, over_keys, ALU.subtract).then_inc(soft, 1)
            dve.wait_ge(exp_ready, 1)
            dve.tensor_reduce(most[:, :], probs_by_head, AX.X, ALU.add).then_inc(soft, 1)
            dve.wait_ge(soft, 3)
            dve.reciprocal(most[:, :], most[:, :]).then_inc(soft, 1)
            dve.wait_ge(soft, 4)
            dve.tensor_tensor(probs_by_head, probs_by_head, over_keys, ALU.mult).then_inc(soft, 1)
            dve.wait_ge(soft, 5)
            dve.wait_ge(bias_added, NT)

            def step(u):
                if within(u):
                    b = u.n % B
                    u.wait(dve, attn_ready, 1, -1)
                    row = Count(u.n // B, u.it, 1)
                    p = bcast(probs[:, bass.ds(row.value(ROW, b * H * B), H * B)], [[1, b + 1], [B, H], [0, DH]])
                    v = rows(u, 2, b)
                    v = bcast(v, [[LT * 3 * D, b + 1], [DH, H], [1, DH]])
                    to = products[u.slot(2)][:, 0:b + 1, :].rearrange("p b (h d) -> p b h d", d=DH)
                    dve.tensor_tensor(to, p, v, ALU.mult).then_inc(weighed, 1)
                    u.wait(dve, weighed, 1, 1)
                    u.wait(dve, a_turned, 1, -1)
                    dve.tensor_reduce(attn[u.slot(2)][:, :], products[u.slot(2)][:, 0:b + 1, :].rearrange("p b n -> p n b"),
                                      AX.X, ALU.add).then_inc(attn_ready, 1)
                m = u.shift(-2)
                if within(m):
                    x = xp[:, bass.ds(tile(m).value(D), D)]
                    m.wait(dve, out_ready, 1, 1)
                    dve.tensor_tensor(x, x, out_ps[m.slot(2)][:, :], ALU.add).then_inc(added, 1)
                    m.wait(dve, added, 1, 1)
                    norm.tile(dve, m, x)
                m = u.shift(-3)
                if within(m):
                    m.wait(dve, h_turned, 1, -1)
                    norm.apply(dve, m, hn[m.slot(2)][:, :], xp[:, bass.ds(tile(m).value(D), D)])

            staged(dve, step, NT, 4, LAG)
            gating.compute(dve, NT, 1.0)


def mix_experts(nc, keep, out, xp, hT, gates, w1, w2, experts_loaded):
    FC = F // P
    H_BANKS = 4
    with Phase(nc, "experts") as ph:
        hidden = [ph.sb(f"hidden{i}", [P, FC, L]) for i in range(2)]
        h_ps = [ph.ps(f"h_ps{i}", [P, L]) for i in range(H_BANKS)]
        y_ps = [[ph.ps(f"y_ps{i}{j}", [P, 2 * D]) for j in range(LT // 2)] for i in range(2)]
        h_ready, hidden_ready, y_ready, mixed = map(ph.sem, ["h_ready", "hidden_ready", "y_ready", "mixed"])
        x_ready, stored = ph.sem("x_ready"), ph.sem("stored")
        block = ph.block()

        def within(n):
            return n.it is not None or 0 <= n.n < B * E

        def tile(n, t):
            return Count(LT * (n.n // E) + t, n.it, LT)

        @block.tensor
        def _(pe):
            pe.wait_ge(experts_loaded, 16 * 2 * E)

            def step(n):
                if within(n):
                    e = n.n % E
                    tokens = bass.ds(tile(n, 0).value(P), L)
                    for f in range(FC):
                        n.wait(pe, hidden_ready, FC, f - H_BANKS + 1)
                        for c in range(KC):
                            mm = pe.matmul(h_ps[f % H_BANKS][:, :], w1[:, e, c, f * P:(f + 1) * P], hT[:, c, tokens],
                                           start=(c == 0), stop=(c == KC - 1))
                        mm.then_inc(h_ready, 1)
                m = n.shift(-1)
                if within(m):
                    e = m.n % E
                    m.wait(pe, hidden_ready, FC, FC)
                    for t in range(LT):
                        if t % 2 == 0:
                            m.wait(pe, mixed, LT, t + 2 - 2 * LT)
                        for f in range(FC):
                            mm = pe.matmul(y_ps[m.slot(2)][t // 2][:, (t % 2) * D:(t % 2 + 1) * D],
                                           hidden[m.slot(2)][:, f, t * P:(t + 1) * P], w2[:, e, f, :],
                                           start=(f == 0), stop=(f == FC - 1))
                        mm.then_inc(y_ready, 1)

            staged(pe, step, B * E, E, 1)

        @block.scalar
        def _(act):
            def step(n):
                if not within(n):
                    return
                for f in range(FC):
                    n.wait(act, h_ready, FC, f + 1)
                    if f == 0:
                        n.wait(act, y_ready, LT, -LT)
                    act.activation(hidden[n.slot(2)][:, f, :], h_ps[f % H_BANKS][:, :], ACT.Gelu).then_inc(hidden_ready, 1)

            staged(act, step, B * E, E, 0)

        @block.vector
        def _(dve):
            def step(n):
                if not within(n):
                    return
                e = n.n % E
                for t in range(LT):
                    x = xp[:, bass.ds(tile(n, t).value(D), D)]
                    gate = gates[:, bass.ds(tile(n, t).value(), 1), e:e + 1].rearrange("p o e -> p (o e)")
                    if t % 2 == 0:
                        n.wait(dve, y_ready, LT, t + 2)
                    if e > 0:
                        n.wait(dve, mixed, LT, t - LT + 1)
                    dve.scalar_tensor_tensor(out=x, in0=y_ps[n.slot(2)][t // 2][:, (t % 2) * D:(t % 2 + 1) * D],
                                             scalar=gate, in1=x, op0=ALU.mult, op1=ALU.add).then_inc(mixed, 1)
                if e == E - 1:
                    n.wait(dve, mixed, LT, LT)
                    at = bass.ds(tile(n, 0).value(D), LT * D)
                    dve.scalar_tensor_tensor(out=keep.x[:, at], in0=xp[:, at], scalar=keep.tanh_g[:, 3:4],
                                             in1=keep.x[:, at], op0=ALU.mult, op1=ALU.add).then_inc(x_ready, 1)

            staged(dve, step, B * E, E, 0)

        @block.sync
        def _(sp):
            with sp.Fori(0, B) as it:
                b = Count(0, it, 1)
                b.wait(sp, x_ready, 1, 1)
                src = keep.x[:, bass.ds(b.value(LT * D), LT * D)].rearrange("p (t d) -> p t d", d=D)
                dst = out[bass.ds(b.value(L), L), :].rearrange("(t p) d -> p t d", p=P)
                sp.dma_start(dst, src).then_inc(stored, 16)
            sp.wait_ge(stored, 16 * B)


class Shared:
    pass


def program(nc, io, out):
    scr, keep = Shared(), Shared()

    def dram(name, shape, dt):
        return nc.dram_tensor(f"scr_{name}", shape, dt).ap()

    rows = HG * DH
    scr.qw, scr.qr, scr.k0, scr.q1, scr.k1 = [dram(name, [NG, PARTS, rows, L], BF16)
                                              for name in ("qw", "qr", "k0", "q1", "k1")]
    scr.pe = dram("pe", [H // HG, PARTS, rows, L], BF16)
    scr.mask = dram("mask", [2, B, L], BF16)
    scr.v0, scr.v1 = [dram(name, [B, H // HG, P, LT, HG * 32], F32) for name in ("v0", "v1")]
    scr.rel = [[dram(f"rel{s}{t}", [2, P, P * (t + 2)], F32) for t in range(LT)] for s in range(REL_SLOTS)]
    scr.o = dram("o", [NG, P, L], F32)
    scr.xT = dram("xT", [NT, P, KC * P], F32)

    with Phase(nc, "keep") as kp:
        keep.ident = kp.sb("ident", [P, P])
        keep.identb = kp.sb("identb", [P, P], BF16)
        keep.tanh_g = kp.sb("tanh_g", [P, 4])
        keep.x = kp.sb("x", [P, NT * D])
        keep.negs, keep.negs_written = kp.sb("negs", [P, 2 * P]), kp.sem("negs_written")
        constants(nc, io, keep, scr)
        project_context(nc, io, keep, scr)
        project_queries(nc, io, keep, scr, "queries0", True, io["L0_WqT"],
                        [(scr.qw, DH ** -0.5, [io["L0_bq"], io["r_w_bias"]]), (scr.qr, DH ** -0.5, [io["L0_bq"], io["r_r_bias"]])])
        attention(nc, io, keep, scr, "attn0", scr.qw, scr.k0, scr.v0, relative=True)
        first_mixture(nc, io, keep, scr)
        project_queries(nc, io, keep, scr, "queries1", False, io["L1_WqT"], [(scr.q1, D ** -0.5, [])])
        attention(nc, io, keep, scr, "attn1", scr.q1, scr.k1, scr.v1, relative=False)
        second_mixture(nc, io, keep, scr, out)


def _layout(i):
    def t(name):
        return i[name].T

    def by_dim(a):
        s = a.shape[:-1]
        return a.reshape(*s, H // HG, HG, DH).swapaxes(-1, -2).reshape(*s, D)

    return {
        "x": i["x"].reshape(B * L, D), "ctx_T": i["ctx_1024"].reshape(B * L, D).T, "mask": i["mask_BxS2_ik0"],
        "g_xattn": i["g_xattn"], "g_ffn": i["g_ffn"], "pos_T": t("L0_xattn_pos_enc"),
        "L0_WqT": by_dim(t("L0_xattn_Wq")), "L0_bq": by_dim(i["L0_xattn_bq"]), "L0_WkT": by_dim(t("L0_xattn_Wk")), "L0_bk": by_dim(i["L0_xattn_bk"]),
        "L0_WvT": t("L0_xattn_Wv"), "L0_bv": i["L0_xattn_bv"], "L0_WoT": t("L0_xattn_Wo"), "L0_bo": i["L0_xattn_bo"],
        "r_w_bias": by_dim(i["L0_xattn_r_w_bias"].reshape(D)), "r_r_bias": by_dim(i["L0_xattn_r_r_bias"].reshape(D)),
        "r_kernel": by_dim(i["L0_xattn_r_kernel"].transpose(1, 0, 2).reshape(D, D)),
        "L0_Wr": i["L0_ffn_Wr"], "L0_WiT": i["L0_ffn_Wi"].transpose(0, 2, 1), "L0_Wo": i["L0_ffn_Wo"],
        "L1_WqT": by_dim(t("L1_xattn_Wq")), "L1_WkT": by_dim(t("L1_xattn_Wk")), "L1_WvT": t("L1_xattn_Wv"), "L1_WoT": t("L1_xattn_Wo"),
        "ln1_w": i["L1_ffn_ln1_w"], "ln1_b": i["L1_ffn_ln1_b"], "in_WT": t("L1_ffn_in_proj_w"), "in_b": i["L1_ffn_in_proj_b"],
        "out_WT": t("L1_ffn_out_proj_w"), "out_b": i["L1_ffn_out_proj_b"], "ln2_w": i["L1_ffn_ln2_w"],
        "ln2_b": i["L1_ffn_ln2_b"], "router_T": t("L1_ffn_router_w"), "w1": i["L1_ffn_w1"], "w2": i["L1_ffn_w2"],
    }


def kernel(**inputs):
    import numpy as _np
    import concourse.bacc as _bacc
    from concourse.bass_utils import run_bass_kernel_spmd as _run

    nc = _bacc.Bacc("TRN2", target_bir_lowering=False, num_devices=1)
    arrays, tensors = {}, {}
    for name, a in _layout({k: _np.asarray(v) for k, v in inputs.items()}).items():
        a = _np.ascontiguousarray(a)
        arrays[f"in_{name}"] = a
        tensors[name] = nc.dram_tensor(f"in_{name}", a.shape, mybir.dt.from_np(a.dtype), kind="ExternalInput").ap()
    out = nc.dram_tensor("out_x", (B * L, D), F32, kind="ExternalOutput").ap()
    program(nc, tensors, out)
    r = _run(nc, [arrays], core_ids=[0])
    return r.results[0]["out_x"].reshape(B, L, D)
```
